# Optimizing a Trainium2 kernel written in Bass

```python
import numpy as np
import jax
import jax.numpy as jnp

def _softmax(x, axis=-1):
    return jax.nn.softmax(x, axis=axis)

def _gelu(x):
    return jax.nn.gelu(x, approximate=True)

def _silu(x):
    return jax.nn.silu(x)

def _sigmoid(x):
    return jax.nn.sigmoid(x)

def _layernorm(x, axis=-1, eps=1e-05):
    m = jnp.mean(x, axis=axis, keepdims=True)
    v = jnp.var(x, axis=axis, keepdims=True)
    return (x - m) / jnp.sqrt(v + eps)

def _scatter_add(tgt, idx, src, axis=0):
    return tgt.at[idx].add(src)

def _segment_sum(src, seg, n):
    return jax.ops.segment_sum(src, seg, n)
kernel_name = 'mk_adj_resnorm_d4_adj_r2_6266d7'

def setup_inputs(seed: int=0):
    np.random.seed(seed)
    _w = jnp.asarray

    def _rec_inputs():
        import jax
        import jax.numpy as jnp
        _gk = jax.random.key(seed)
        x = 7.22e-05 + 1 * jax.random.normal(jax.random.fold_in(_gk, 1), (64, 128, 256), jnp.float32)
        _w = (1.0 + jnp.arange(128, dtype=jnp.float32)) ** (-0.5)
        _w = _w / _w.mean()
        _pij = jnp.clip(0.03125 * _w[:, None] * _w[None, :], 0.0, 1.0)
        _a = jax.random.uniform(jax.random.fold_in(_gk, 2), (128, 128)) < _pij
        _a = jnp.logical_or(_a, jnp.swapaxes(_a, -1, -2))
        _a = jnp.logical_or(_a, jnp.eye(128, dtype=bool))
        _af = _a.astype(jnp.float32)
        _af = _af * jax.random.uniform(jax.random.fold_in(_gk, 3), (128, 128), jnp.float32, 0.05, 0.00390622)
        adj = _af
        return (x, adj)
    x, adj = _rec_inputs()

    def _L0_gnn_setup():
        import jax, jax.numpy as jnp
        import numpy as np
        B, N, D, T = (64, 128, 256, 3)

        def _lin(v, W, b):
            return jnp.einsum('...i,oi->...o', v, W) + b
        key = jax.random.key(seed)
        ks = jax.random.split(key, 12)
        s2 = 1.0 / np.sqrt(2 * D)
        s1 = 1.0 / np.sqrt(D)
        return {'x': jax.random.normal(ks[0], (B, N, D), jnp.float32), 'in_mat': jax.random.uniform(ks[1], (N, N), jnp.float32) / N, 'out_mat': jax.random.uniform(ks[2], (N, N), jnp.float32) / N, 'w3_w': jax.random.normal(ks[3], (D, 2 * D), jnp.float32) * s2, 'w3_b': jnp.zeros((D,), jnp.float32), 'u3_w': jax.random.normal(ks[4], (D, D), jnp.float32) * s1, 'u3_b': jnp.zeros((D,), jnp.float32), 'w4_w': jax.random.normal(ks[5], (D, 2 * D), jnp.float32) * s2, 'w4_b': jnp.zeros((D,), jnp.float32), 'w5_w': jax.random.normal(ks[6], (D, 2 * D), jnp.float32) * s2, 'w5_b': jnp.zeros((D,), jnp.float32), 'u5_w': jax.random.normal(ks[7], (D, D), jnp.float32) * s1, 'u5_b': jnp.zeros((D,), jnp.float32)}
    _L0_gnn_all = _L0_gnn_setup()
    _L0_gnn_in = {k: v for k, v in _L0_gnn_all.items() if k in ('w3_w', 'w3_b', 'u3_w', 'u3_b', 'w4_w', 'w4_b', 'w5_w', 'w5_b', 'u5_w', 'u5_b')}
    del _L0_gnn_all

    def _L1_gnn_setup():
        import jax, jax.numpy as jnp
        import numpy as np
        B, N, D = (8, 1024, 256)
        key = jax.random.key(seed)
        k1, k2, k3, k4, k5 = jax.random.split(key, 5)
        neuron_states = jax.random.normal(k1, (B, N, D), dtype=jnp.float32)
        adjacency = jax.random.randint(k2, (N, N), 0, 2).astype(jnp.float32)
        scale = 1.0 / np.sqrt(D)
        Wq = jax.random.normal(k3, (D, D), dtype=jnp.float32) * scale
        Wk = jax.random.normal(k4, (D, D), dtype=jnp.float32) * scale
        Wv = jax.random.normal(k5, (D, D), dtype=jnp.float32) * scale
        return {'neuron_states': neuron_states, 'adjacency': adjacency, 'Wq': Wq, 'Wk': Wk, 'Wv': Wv}
    _L1_gnn_all = _L1_gnn_setup()
    _L1_gnn_in = {k: v for k, v in _L1_gnn_all.items() if k in ('Wq', 'Wk', 'Wv')}
    del _L1_gnn_all

    def _L2_gnn_setup():
        import jax, jax.numpy as jnp
        import numpy as np
        B, N, D, H = (16, 1025, 256, 8)
        LN_EPS = 1e-05

        def _make_mask(key, n):
            n_proto = n - 1
            adj = jax.random.bernoulli(key, 0.03, (n_proto, n_proto)).astype(jnp.float32)
            adj = jnp.clip(adj + adj.T + jnp.eye(n_proto, dtype=jnp.float32), 0.0, 1.0)
            mask = jnp.zeros((n, n), dtype=jnp.float32)
            mask = mask.at[0, :].set(1.0).at[:, 0].set(1.0)
            mask = mask.at[1:, 1:].set(adj)
            return mask
        key = jax.random.key(seed)
        ks = jax.random.split(key, 7)
        s = 1.0 / np.sqrt(D)
        return {'x': jax.random.normal(ks[0], (B, N, D), dtype=jnp.float32), 'w_qkv': jax.random.uniform(ks[1], (D, 3 * D), dtype=jnp.float32, minval=-s, maxval=s), 'w_proj': jax.random.uniform(ks[2], (D, D), dtype=jnp.float32, minval=-s, maxval=s), 'b_proj': jnp.zeros((D,), dtype=jnp.float32), 'ln_gamma': jnp.ones((D,), dtype=jnp.float32), 'ln_beta': jnp.zeros((D,), dtype=jnp.float32), 'attn_mask': _make_mask(ks[3], N)}
    _L2_gnn_all = _L2_gnn_setup()
    _L2_gnn_in = {k: v for k, v in _L2_gnn_all.items() if k in ('w_qkv', 'w_proj', 'b_proj', 'ln_gamma', 'ln_beta')}
    del _L2_gnn_all

    def _L3_gnn_setup():
        import jax, jax.numpy as jnp
        import numpy as np
        ALPHA = 0.2
        key = jax.random.key(seed)
        k0, k1, k2, k3 = jax.random.split(key, 4)
        B, N, C, F = (64, 512, 256, 256)
        x = jax.random.normal(k0, (B, N, C), dtype=jnp.float32)
        W = jax.random.normal(k1, (C, F), dtype=jnp.float32) * (1.414 / np.sqrt(C + F))
        a = jax.random.normal(k2, (2 * F, 1), dtype=jnp.float32) * (1.414 / np.sqrt(2 * F + 1))
        beta = jnp.ones((1,), dtype=jnp.float32)
        mask = (jax.random.uniform(k3, (N, N)) < 0.3).astype(jnp.float32)
        return {'x': x, 'W': W, 'a': a, 'beta': beta, 'mask': mask}
    _L3_gnn_all = _L3_gnn_setup()
    _L3_gnn_in = {k: v for k, v in _L3_gnn_all.items() if k in ('W', 'a', 'beta')}
    del _L3_gnn_all
    return {'x': x, 'adj': adj, 'L0_gnn_w3_w': _L0_gnn_in['w3_w'], 'L0_gnn_w3_b': _L0_gnn_in['w3_b'], 'L0_gnn_u3_w': _L0_gnn_in['u3_w'], 'L0_gnn_u3_b': _L0_gnn_in['u3_b'], 'L0_gnn_w4_w': _L0_gnn_in['w4_w'], 'L0_gnn_w4_b': _L0_gnn_in['w4_b'], 'L0_gnn_w5_w': _L0_gnn_in['w5_w'], 'L0_gnn_w5_b': _L0_gnn_in['w5_b'], 'L0_gnn_u5_w': _L0_gnn_in['u5_w'], 'L0_gnn_u5_b': _L0_gnn_in['u5_b'], 'L1_gnn_Wq': _L1_gnn_in['Wq'], 'L1_gnn_Wk': _L1_gnn_in['Wk'], 'L1_gnn_Wv': _L1_gnn_in['Wv'], 'L2_gnn_w_qkv': _L2_gnn_in['w_qkv'], 'L2_gnn_w_proj': _L2_gnn_in['w_proj'], 'L2_gnn_b_proj': _L2_gnn_in['b_proj'], 'L2_gnn_ln_gamma': _L2_gnn_in['ln_gamma'], 'L2_gnn_ln_beta': _L2_gnn_in['ln_beta'], 'L3_gnn_W': _L3_gnn_in['W'], 'L3_gnn_a': _L3_gnn_in['a'], 'L3_gnn_beta': _L3_gnn_in['beta']}

def reference(x, adj, L0_gnn_w3_w, L0_gnn_w3_b, L0_gnn_u3_w, L0_gnn_u3_b, L0_gnn_w4_w, L0_gnn_w4_b, L0_gnn_w5_w, L0_gnn_w5_b, L0_gnn_u5_w, L0_gnn_u5_b, L1_gnn_Wq, L1_gnn_Wk, L1_gnn_Wv, L2_gnn_w_qkv, L2_gnn_w_proj, L2_gnn_b_proj, L2_gnn_ln_gamma, L2_gnn_ln_beta, L3_gnn_W, L3_gnn_a, L3_gnn_beta):
    import jax
    import jax.numpy as jnp

    def _L0_gnn_ref(x, in_mat, out_mat, w3_w, w3_b, u3_w, u3_b, w4_w, w4_b, w5_w, w5_b, u5_w, u5_b):
        import jax, jax.numpy as jnp
        import numpy as np
        B, N, D, T = (64, 128, 256, 3)

        def _lin(v, W, b):
            return jnp.einsum('...i,oi->...o', v, W) + b
        h = x
        for _ in range(T):
            a_in = jnp.einsum('nm,bmd->bnd', in_mat, h)
            a_out = jnp.einsum('nm,bmd->bnd', out_mat, h)
            av = jnp.concatenate([a_in, a_out], axis=-1)
            z = jax.nn.sigmoid(_lin(av, w3_w, w3_b) + _lin(h, u3_w, u3_b))
            r = jax.nn.sigmoid(_lin(av, w4_w, w4_b) + _lin(h, u3_w, u3_b))
            hv = jnp.tanh(_lin(av, w5_w, w5_b) + _lin(r * h, u5_w, u5_b))
            h = (1.0 - z) * h + z * hv
        return h

    def _L1_gnn_ref(neuron_states, adjacency, Wq, Wk, Wv):
        import jax, jax.numpy as jnp
        import numpy as np
        B, N, D = (8, 1024, 256)
        q = jnp.einsum('bnd,ed->bne', neuron_states, Wq)
        k = jnp.einsum('bnd,ed->bne', neuron_states, Wk)
        v = jnp.einsum('bnd,ed->bne', neuron_states, Wv)
        rel = jnp.einsum('bnd,bmd->bnm', q, k)
        rel = adjacency.T[None, :, :] * rel
        rel = rel / jnp.linalg.norm(rel, axis=2, keepdims=True)
        return jnp.einsum('bnm,bmd->bnd', rel, v)

    def _L2_gnn_ref(x, w_qkv, w_proj, b_proj, ln_gamma, ln_beta, attn_mask):
        import jax, jax.numpy as jnp
        import numpy as np
        B, N, D, H = (16, 1025, 256, 8)
        LN_EPS = 1e-05

        def _make_mask(key, n):
            n_proto = n - 1
            adj = jax.random.bernoulli(key, 0.03, (n_proto, n_proto)).astype(jnp.float32)
            adj = jnp.clip(adj + adj.T + jnp.eye(n_proto, dtype=jnp.float32), 0.0, 1.0)
            mask = jnp.zeros((n, n), dtype=jnp.float32)
            mask = mask.at[0, :].set(1.0).at[:, 0].set(1.0)
            mask = mask.at[1:, 1:].set(adj)
            return mask
        b, n, d = x.shape
        hd = d // H
        scale = hd ** (-0.5)
        qkv = (x @ w_qkv).reshape(b, n, 3, H, hd).transpose(2, 0, 3, 1, 4)
        q, k, v = (qkv[0], qkv[1], qkv[2])
        attn = jnp.einsum('bhnd,bhmd->bhnm', q, k) * scale
        attn = jnp.where(attn_mask[None, None] == 0, -jnp.inf, attn)
        attn = jax.nn.softmax(attn, axis=-1)
        o = jnp.einsum('bhnm,bhmd->bhnd', attn, v).transpose(0, 2, 1, 3).reshape(b, n, d)
        o = o @ w_proj + b_proj
        mu = jnp.mean(o, axis=-1, keepdims=True)
        var = jnp.mean(jnp.square(o - mu), axis=-1, keepdims=True)
        ln = (o - mu) * jax.lax.rsqrt(var + LN_EPS) * ln_gamma + ln_beta
        return o + ln

    def _L3_gnn_ref(x, W, a, beta, mask):
        import jax, jax.numpy as jnp
        import numpy as np
        ALPHA = 0.2
        F_ = W.shape[1]
        h = jnp.einsum('bnc,cf->bnf', x, W)
        a1, a2 = (a[:F_, 0], a[F_:, 0])
        s1 = jnp.einsum('bnf,f->bn', h, a1)
        s2 = jnp.einsum('bnf,f->bn', h, a2)
        e = jax.nn.leaky_relu(s1[:, :, None] + s2[:, None, :], negative_slope=ALPHA)
        e = e * mask[None, :, :]
        att = jax.nn.softmax(e, axis=2)
        h_prime = jnp.einsum('bij,bjf->bif', att, h)
        return jax.nn.elu(h_prime + beta * h)
    x = _layernorm(x + _L0_gnn_ref(x, adj, adj, L0_gnn_w3_w, L0_gnn_w3_b, L0_gnn_u3_w, L0_gnn_u3_b, L0_gnn_w4_w, L0_gnn_w4_b, L0_gnn_w5_w, L0_gnn_w5_b, L0_gnn_u5_w, L0_gnn_u5_b), axis=-1)
    x = _layernorm(x + _L1_gnn_ref(x, adj, L1_gnn_Wq, L1_gnn_Wk, L1_gnn_Wv), axis=-1)
    x = _layernorm(x + _L2_gnn_ref(x, L2_gnn_w_qkv, L2_gnn_w_proj, L2_gnn_b_proj, L2_gnn_ln_gamma, L2_gnn_ln_beta, adj), axis=-1)
    x = _layernorm(x + _L3_gnn_ref(x, L3_gnn_W, L3_gnn_a, L3_gnn_beta, adj), axis=-1)
    return x

_drawn_inputs = setup_inputs


def setup_inputs(seed=0):
    import zlib

    import numpy as np

    out = dict(_drawn_inputs(seed))
    spreads = {'L0_gnn_w3_b': (0.0, 0.351),
     'L0_gnn_u3_b': (0.0, 0.308),
     'L0_gnn_w4_b': (0.0, 0.75),
     'L0_gnn_w5_b': (0.0, 0.1),
     'L0_gnn_u5_b': (0.0, 0.1),
     'L2_gnn_b_proj': (0.0, 0.1),
     'L2_gnn_ln_gamma': (1.0, 0.2),
     'L2_gnn_ln_beta': (0.0, 0.1)}
    factors = {'L0_gnn_w4_w': 4.735, 'L3_gnn_a': 60.793}
    for name, (base, spread) in spreads.items():
        noise = np.random.default_rng([zlib.crc32(name.encode()), seed]).standard_normal(out[name].shape)
        drawn = base * np.exp(spread * noise) if base else spread * noise
        out[name] = jnp.asarray(drawn.astype(out[name].dtype))
    for name, factor in factors.items():
        out[name] = (out[name] * factor).astype(out[name].dtype)
    return out
```

```python
import concourse.bass as bass
from concourse import mybir
from contextlib import ExitStack

F32 = mybir.dt.float32
F16 = mybir.dt.float16
ALU = mybir.AluOpType
ACT = mybir.ActivationFunctionType
AX = mybir.AxisListType

B, N, D, H = 64, 128, 256, 8
P = 128
GB = 4
NG = B // GB
T = GB * N
KC = D // P
HD = D // H
HC = P // HD
ITERS = 3
EPS = 1e-5
W_SCALE = 16.0
ADJ_SCALE = 64.0
NO_EDGE = -1e30
SLOPE = 0.2

GRU_INIT = [("gru", "init", 0)]


def gru_iter(it):
    return [("gru", s, it) for s in ("spread", "reset", "update", "candidate", "state", "nodes")]


def tail_steps():
    t = [("ln", 0), ("x1T", 0), ("x1T", 1), ("q1T", 0), ("q1T", 1), ("v1", 0), ("v1", 1), ("rel", 0)]
    t += [("out1", b) for b in range(GB)] + [("mix1", 0), ("ln", 1)]
    t += [("x2T", 0), ("x2T", 1), ("q2T", 0), ("q2T", 1), ("k2T", 0), ("k2T", 1), ("v2", 0), ("v2", 1)]
    t += [("score", 0), ("score", 1), ("score", 2), ("score", 3)]
    for b in range(GB):
        t += [("probT", 2 * b), ("probT", 2 * b + 1), ("head_out", b)]
        if b + 2 < GB:
            t += [("score", 2 * b + 4), ("score", 2 * b + 5)]
    t += [("oT", 0), ("oT", 1), ("proj", 0), ("proj", 1), ("ln", 2), ("mix2", 0), ("ln", 3)]
    t += [("x3T", 0), ("x3T", 1)] + [("h3", b) for b in range(GB)]
    t += [("edge", 0), ("edge_soft", 0), ("attT", 0), ("out3", 0), ("out3", 1), ("elu", 0), ("ln", 4), ("store", 0)]
    return [("tail",) + s for s in t]


SLOTS = dict(spread=2, reset=2, update=3, candidate=9, state=0, nodes=5)
PE_TILES = [s[1:] for s in tail_steps() if s[1] not in
            ("ln", "mix1", "mix2", "edge_soft", "elu", "store")]


def body_order():
    tail, out = tail_steps(), []
    per = len(tail) / ITERS / sum(SLOTS.values())
    gru = GRU_INIT + [s for it in range(ITERS) for s in gru_iter(it)]
    due = 0.0
    for s in gru:
        out.append(s)
        due += SLOTS.get(s[1], 0) * per
        while tail and due >= 1:
            out.append(tail.pop(0))
            due -= 1
    return out + tail


class Signal:

    def __init__(self, ctx, nc, name, per_group, step=1, base=0):
        self.sem = ctx.enter_context(nc.semaphore(name))
        self.per_group, self.step = per_group, step
        self.base = base

    def setup(self, eng):
        eng.sem_inc(self.sem, self.base)

    def at(self, g, k):
        return (g * self.per_group + k) * self.step + self.base


def build(nc, x, adj, w3_w, w3_b, u3_w, u3_b, w4_w, w4_b, w5_w, w5_b, u5_w, u5_b, Wq, Wk, Wv,
          w_qkv, w_proj, b_proj, ln_gamma, ln_beta, W3l, a3l, beta3l, out):
    ctx = ExitStack()
    with ctx:
        def sb(name, shape, dt=F32):
            return ctx.enter_context(nc.sbuf_tensor(name, shape, dt))

        def hilo(name, shape):
            return sb(name + "_hi", shape, F16), sb(name + "_lo", shape, F16)

        def sig(name, per_group, step=1, base=0):
            return Signal(ctx, nc, name, per_group, step, base)

        ident = sb("ident", [P, P])
        adj_n = sb("adj_n", [P, N])
        no_edge = sb("no_edge", [P, N])
        half = sb("half", [P, 6 * GB])
        gru_bias = sb("gru_bias", [P, 3, KC])
        bproj_b = sb("bproj_b", [P, D])
        gamma_b = sb("gamma_b", [P, D])
        lnbeta_b = sb("lnbeta_b", [P, D])
        beta_b = sb("beta_b", [P, 1])
        adjT = hilo("adjT", [P, N])
        WR, WZR, WH = hilo("WR", [P, KC, D]), hilo("WZR", [P, KC, D]), hilo("WH", [P, KC, D])
        UG, UH = hilo("UG", [P, KC, D]), hilo("UH", [P, KC, D])
        WQK, WV1 = hilo("WQK", [P, KC, D]), hilo("WV1", [P, KC, D])
        WQ2, WK2, WV2 = hilo("WQ2", [P, KC, D]), hilo("WK2", [P, KC, D]), hilo("WV2", [P, KC, D])
        WP2, WG = hilo("WP2", [P, KC, D]), hilo("WG", [P, KC, D + 2])

        x_in = sb("x_in", [P, GB, D])
        x_keep = sb("x_keep", [P, GB, D])
        hT = sb("hT", [P, KC, T])
        hTs, hNs = hilo("hTs", [P, KC, T]), hilo("hNs", [P, GB, D])
        aTs, rhs_ = hilo("aTs", [P, KC, T]), hilo("rhTs", [P, KC, T])
        t_reset, t_update = sb("t_reset", [P, KC, T]), sb("t_update", [P, KC, T])
        cand, rh2 = sb("cand", [P, KC, T]), sb("rh2", [P, KC, T])
        diff, step_ = sb("diff", [P, KC, T]), sb("step", [P, KC, T])
        gru_out = rh2[:, :, :].rearrange("p c t -> p (c t)").rearrange("p (b d) -> p b d", b=GB)
        y = sb("y", [P, GB, D])
        xs = [sb("x1", [P, GB, D]), sb("x2", [P, GB, D]), sb("x3", [P, GB, D]), sb("x4", [P, GB, D])]
        xTs = hilo("xTs", [P, KC, T])
        q1s = hilo("q1s", [P, KC, T])
        vr = hilo("vr", [P, GB, D + N])
        rm = sb("rm", [P, T])
        u1 = sb("u1", [P, GB, D])
        junk = sb("junk", [P, N])
        norm2 = sb("norm2", [P, GB])
        q2s, k2s = hilo("q2s", [P, KC, T]), hilo("k2s", [P, KC, T])
        v2s = hilo("v2s", [P, GB, D])
        qst, kst = sb("qst", [3 * HD, H, T], F16), sb("kst", [3 * HD, H, T], F16)
        sm = sb("sm", [P, 2, HC * N])
        nmax = sb("nmax", [P, 2 * GB, HC])
        rsum = sb("rsum", [P, 2 * GB, HC])
        rinv = sb("rinv", [P, 2 * GB, HC])
        ex = sb("ex", [P, 4, HC * N])
        pTs = hilo("pTs", [P, 2, H, N])
        o_n = sb("o_n", [P, GB, D])
        oTs = hilo("oTs", [P, KC, T])
        proj_o = sb("proj_o", [P, GB, D])
        base2 = sb("base2", [P, GB, D])
        ln_o = u1
        ln_g = sb("ln_g", [P, GB, D])
        h3f = sb("h3f", [P, GB, D + 2])
        h3s = hilo("h3s", [P, GB, D])
        presum, edge = sm[:, 0, :], sm[:, 1, :]
        enmax, ersum, erinv = sb("enmax", [P, GB]), sb("ersum", [P, GB]), sb("erinv", [P, GB])
        eex = ex[:, 0, :]
        aT3 = hilo("aT3", [P, GB, N])
        bh = o_n
        g3, m3, e3 = proj_o, ln_g, u1
        stats = sb("stats", [P, 5, GB, 6])
        meanvar = sb("meanvar", [P, 5, GB, 2])
        vareps, rstd = sb("vareps", [P, 6, GB]), sb("rstd", [P, 6, GB])

        def bank(name):
            return ctx.enter_context(nc.psum_tensor(name, [P, 512], F32))
        SA = [bank(f"SA{i}") for i in range(2)]
        SG = [bank(f"SG{i}") for i in range(2)]
        SC = [bank(f"SC{i}") for i in range(2)]
        ST = [bank(f"ST{i}") for i in range(2)]

        w_in, consts = sig("w_in", 0, 16), sig("consts", 0)
        prep, wps, whi, wlo = sig("prep", 0), sig("wps", 0), sig("whi", 0), sig("wlo", 0)
        x_loaded = sig("x_loaded", 1, 16)
        x_freed = sig("x_freed", 1)
        xT_ps, hT0 = sig("xT_ps", KC), sig("hT0", KC)
        hT_hi, hT_lo = sig("hT_hi", KC * ITERS), sig("hT_lo", KC * ITERS)
        hN_hi, hN_lo = sig("hN_hi", 2 * ITERS), sig("hN_lo", 2 * ITERS)
        a_ps, a_hi, a_lo = sig("a_ps", 6), sig("a_hi", 6), sig("a_lo", 6)
        r_ps, r_t, rh_f, rh_hi, rh_lo = (sig(n, 6) for n in ("r_ps", "r_t", "rh_f", "rh_hi", "rh_lo"))
        z_ps, z_t, c_ps, c_t = (sig(n, 6) for n in ("z_ps", "z_t", "c_ps", "c_t"))
        d_f, u_f, h_new, hN_ps = (sig(n, 6) for n in ("d_f", "u_f", "h_new", "hN_ps"))
        y0 = sig("y0", 2)
        tile_ps = sig("tile_ps", len(PE_TILES))
        ln_stats, ln_aggr, ln_ve, ln_rstd, ln_out = (sig("ln_stats", 20), sig("ln_aggr", 20), sig("ln_ve", 5),
                                                     sig("ln_rstd", 5), sig("ln_out", 20))
        x_hi, x_lo = sig("x_hi", 3 * KC), sig("x_lo", 3 * KC)
        q1_hi, q1_lo, v1_hi, v1_lo = (sig(n, 2) for n in ("q1_hi", "q1_lo", "v1_hi", "v1_lo"))
        rm_f, rm_hi, rm_lo = (sig(n, 1) for n in ("rm_f", "rm_hi", "rm_lo"))
        u1_f, n2_f, rn_f, y1_f = sig("u1_f", GB), sig("n2_f", GB), sig("rn_f", 1), sig("y1_f", GB)
        q2_hi, q2_lo, k2_hi, k2_lo, v2_hi, v2_lo = (sig(n, 2) for n in
                                                    ("q2_hi", "q2_lo", "k2_hi", "k2_lo", "v2_hi", "v2_lo"))
        stacked = sig("stacked", 6 * HC, 16)
        sm_f, nmax_f, ex_f = sig("sm_f", 8), sig("nmax_f", 8), sig("ex_f", 8)
        pT_hi, pT_lo = sig("pT_hi", 8), sig("pT_lo", 8)
        rinv_f, o_f = sig("rinv_f", GB), sig("o_f", GB)
        oT_hi, oT_lo, proj_f = sig("oT_hi", 2), sig("oT_lo", 2), sig("proj_f", 2)
        base_f, baseo_f, lng_f, y2_f = sig("base_f", 1), sig("baseo_f", 1), sig("lng_f", 1), sig("y2_f", 1)
        h3_f, h3_hi, h3_lo, bh_f = sig("h3_f", GB), sig("h3_hi", 1), sig("h3_lo", 1), sig("bh_f", 1)
        presum_f, edge_f, enmax_f, eex_f, erinv_f = (sig("presum_f", 1), sig("edge_f", 2), sig("enmax_f", 1),
                                                    sig("eex_f", 1), sig("erinv_f", 1))
        a3_hi, a3_lo, g3_f, m3_f, e3_f, p3_f, y3_f = (sig("a3_hi", 1), sig("a3_lo", 1), sig("g3_f", GB, base=GB),
                                                      sig("m3_f", 1), sig("e3_f", 1), sig("p3_f", 1), sig("y3_f", 1))
        stored = sig("stored", 1, 16, base=16)

        TILE = {name: i for i, name in enumerate(PE_TILES)}
        FREED = {}
        for c in range(2):
            FREED["x1T", c], FREED["x2T", c], FREED["x3T", c] = (x_lo, c + 1), (x_lo, c + 3), (x_lo, c + 5)
            FREED["q1T", c], FREED["v1", c] = (q1_lo, c + 1), (v1_lo, c + 1)
            FREED["q2T", c], FREED["k2T", c], FREED["v2", c] = (q2_lo, c + 1), (k2_lo, c + 1), (v2_lo, c + 1)
            FREED["oT", c], FREED["proj", c], FREED["out3", c] = (oT_lo, c + 1), (proj_f, c + 1), (g3_f, 2 * c + 2)
        for b in range(GB):
            FREED["out1", b], FREED["head_out", b], FREED["h3", b] = (n2_f, b + 1), (o_f, b + 1), (h3_f, b + 1)
        for s in range(2 * GB):
            FREED["score", s], FREED["probT", s] = (sm_f, s + 1), (pT_lo, s + 1)
        FREED["rel", 0], FREED["edge", 0], FREED["attT", 0] = (rm_f, 1), (presum_f, 1), (a3_lo, 1)

        def tile(name, k):
            return ST[TILE[name, k] % 2]

        def tile_full(eng, g, name, k):
            eng.wait_ge(tile_ps.sem, tile_ps.at(g, TILE[name, k] + 1))

        def wait(eng, s, g, k):
            eng.wait_ge(s.sem, s.at(g, k))

        passed = sig("passed", 0)

        def gate(eng, s, g, k):
            wait(eng, s, g, k)
            eng.sem_inc(passed.sem, 1)

        stage = {}

        def staged(name, home, cols):
            stage[name] = home.rearrange("p a b -> p (a b)")[:, 0:KC * cols].rearrange("p (k d) -> p k d", k=KC)
            return stage[name]

        LOADS = [(staged("w3", t_reset, 2 * D), w3_w), (staged("w4", t_update, 2 * D), w4_w),
                 (staged("w5", cand, 2 * D), w5_w), (staged("u3", rh2, D), u3_w), (staged("u5", diff, D), u5_w),
                 (staged("Wq", step_, D), Wq), (staged("Wk", xs[0], D), Wk), (staged("Wv", xs[1], D), Wv),
                 (staged("wp", xs[3], D), w_proj), (staged("wg", y, D), W3l)]
        qkv_home = ex[:, :, :].rearrange("p a b -> p (a b)")[:, 0:KC * 3 * D].rearrange("p (k d) -> p k d", k=KC)
        a_bc = u1[:, 0:2, :]
        bias_in = sb("bias_in", [P, 5, KC])
        wr_f, wzr_f, wh_f = o_n[:, 0:2, :], proj_o[:, 0:2, :], base2[:, 0:2, :]
        wa_f = sb("wa_f", [P, KC, 2])
        wa_t = ln_g[:, :, :]
        N_LOADS = len(LOADS) + 1 + 1 + 5 + 3 + 1 + 2
        PREPARED = {}
        PREP_COUNT = 13
        WT = [(adjT, "adj", ADJ_SCALE, N), (WR, "wr", W_SCALE, D), (WZR, "wzr", W_SCALE, D), (WH, "wh", W_SCALE, D),
              (UG, "u3", W_SCALE, D), (UH, "u5", W_SCALE / 2, D), (WV1, "Wv", W_SCALE, D), (WQK, "qk", W_SCALE, D)]
        WN = [(WQ2, qkv_home[:, :, 0:D], W_SCALE * HD ** -0.5), (WK2, qkv_home[:, :, D:2 * D], W_SCALE),
              (WV2, qkv_home[:, :, 2 * D:3 * D], W_SCALE), (WP2, stage["wp"], W_SCALE),
              ((WG[0][:, :, 0:D], WG[1][:, :, 0:D]), stage["wg"], W_SCALE),
              ((WG[0][:, :, D:D + 2], WG[1][:, :, D:D + 2]), wa_f, W_SCALE)]

        block = ctx.enter_context(nc.Block())

        def x_of(g, src):
            return src[bass.ds(g * GB, GB)].rearrange("b n d -> n b d")

        def run_all(eng, gru, tail):
            for s in GRU_INIT + [s for it in range(ITERS) for s in gru_iter(it)]:
                gru(s[1], s[2], 0)
            with eng.Fori(0, NG - 1) as g:
                for kind, name, k in body_order():
                    if kind == "gru":
                        gru(name, k, g + 1)
                    else:
                        tail(name, k, g)
            for s in tail_steps():
                tail(s[1], s[2], NG - 1)

        @block.sync
        def _(sp):
            nc_dma = [(adj_n[:, :], adj)]
            nc_dma += [(dst, src.rearrange("(k p) d -> p k d", p=P)) for dst, src in LOADS]
            nc_dma += [(qkv_home, w_qkv.rearrange("(k p) d -> p k d", p=P))]
            nc_dma += [(bproj_b[:, :], b_proj.rearrange("(a d) -> a d", a=1).broadcast_to([P, D])),
                       (gamma_b[:, :], ln_gamma.rearrange("(a d) -> a d", a=1).broadcast_to([P, D])),
                       (lnbeta_b[:, :], ln_beta.rearrange("(a d) -> a d", a=1).broadcast_to([P, D])),
                       (beta_b[:, :], beta3l.rearrange("(a d) -> a d", a=1).broadcast_to([P, 1]))]
            nc_dma += [(a_bc[:, i, :], a3l[i * D:(i + 1) * D, :].rearrange("d a -> a d").broadcast_to([P, D]))
                       for i in range(2)]
            with nc.allow_non_contiguous_dma("biases, one element per partition"):
                nc_dma += [(bias_in[:, i, :], v.rearrange("(k p) -> p k", p=P))
                           for i, v in enumerate((w3_b, u3_b, w4_b, w5_b, u5_b))]
                assert len(nc_dma) == N_LOADS
                for dst, src in nc_dma:
                    sp.dma_start(dst, src).then_inc(w_in.sem, 16)

            def load_x(g, first=False):
                if not first:
                    wait(sp, x_freed, g - 1, 1)
                    wait(sp, xT_ps, g - 1, KC)
                    wait(sp, hN_lo, g - 1, 2)
                sp.dma_start(x_in[:, :, :], x_of(g, x)).then_inc(x_loaded.sem, 16)

            def stack(g):
                for j in range(HC):
                    for dst, src, parts, lo_done in ((qst, q2s, (0, 0, 1), q2_lo), (kst, k2s, (0, 1, 0), k2_lo)):
                        if j == 0:
                            wait(sp, lo_done, g, 2)
                        for r, part in enumerate(parts):
                            d = dst[HD * r:HD * (r + 1), :, :].rearrange("p (c j) t -> p c j t", j=HC)[:, :, j, :]
                            sp.dma_start(d, src[part][HD * j:HD * (j + 1), :, :]).then_inc(stacked.sem, 16)

            def store(g):
                wait(sp, ln_out, g, 20)
                sp.dma_start(x_of(g, out), xs[3][:, :, :]).then_inc(stored.sem, 16)

            stored.setup(sp)
            load_x(0, first=True)
            load_x(1)
            with sp.Fori(0, NG - 2) as g:
                stack(g)
                load_x(g + 2)
                store(g)
            for g in (NG - 2, NG - 1):
                stack(g)
                store(g)
            wait(sp, stored, NG - 1, 1)

        @block.gpsimd
        def _(pool):
            pool.memset(ident[:, :], 0.0).then_inc(consts.sem, 1)
            pool.memset(half[:, :], -0.5).then_inc(consts.sem, 1)
            pool.wait_ge(consts.sem, 2)
            pool.affine_select(out=ident[:, :], in_=ident[:, :], compare_op=ALU.not_equal, fill=1.0, base=0,
                               pattern=[[-1, P]], channel_multiplier=1).then_inc(consts.sem, 1)
            pool.wait_ge(consts.sem, 3)

            def gru(step, it, g):
                if step == "init":
                    for c in range(KC):
                        wait(pool, hT_hi, g, c + 1)
                        pool.tensor_tensor(hTs[1][:, c, :], hT[:, c, :], hTs[0][:, c, :], ALU.subtract)\
                            .then_inc(hT_lo.sem, 1)
                if step == "candidate":
                    for c in range(KC):
                        wait(pool, c_t, g, KC * it + c + 1)
                        pool.tensor_tensor(diff[:, c, :], cand[:, c, :], hT[:, c, :], ALU.subtract)\
                            .then_inc(d_f.sem, 1)
                if step == "state" and it + 1 < ITERS:
                    for c in range(KC):
                        wait(pool, hT_hi, g, KC * (it + 1) + c + 1)
                        pool.tensor_tensor(hTs[1][:, c, :], hT[:, c, :], hTs[0][:, c, :], ALU.subtract)\
                            .then_inc(hT_lo.sem, 1)

            def tail(step, k, g):
                if step == "ln":
                    wait(pool, ln_ve, g, k + 1)
                    pool.tensor_tensor(rstd[:, k, :], vareps[:, k, :], half[:, 0:GB], ALU.pow).then_inc(ln_rstd.sem, 1)
                    if k == 1:
                        wait(pool, ln_out, g, 8)
                        lb = lnbeta_b[:, :].rearrange("p (a d) -> p a d", a=1).broadcast_to([P, GB, D])
                        pool.tensor_tensor(base2[:, :, :], xs[1][:, :, :], lb, ALU.add).then_inc(base_f.sem, 1)
                if step == "mix1":
                    wait(pool, n2_f, g, GB)
                    pool.tensor_tensor(rstd[:, 5, :], norm2[:, :], half[:, 0:GB], ALU.pow).then_inc(rn_f.sem, 1)
                if step == "mix2":
                    wait(pool, proj_f, g, 2)
                    wait(pool, base_f, g, 1)
                    pool.tensor_tensor(base2[:, :, :], base2[:, :, :], proj_o[:, :, :], ALU.add).then_inc(baseo_f.sem, 1)
                if step == "edge":
                    gate(pool, h3_f, g, GB)
                    pool.tensor_scalar(bh[:, :, :], h3f[:, :, 0:D], beta_b[:, 0:1], 0.0, ALU.mult, ALU.add)\
                        .then_inc(bh_f.sem, 1)

            pool.wait_ge(w_in.sem, 16 * N_LOADS)
            pool.wait_ge(wlo.sem, len(WT) + len(WN))
            run_all(pool, gru, tail)

        @block.tensor
        def _(pe):
            def mm3(dst, lhsT, rhs, first, last, again=False):
                pe.matmul(dst, lhsT[0], rhs[0], start=first, stop=False, skip_group_check=again)
                pe.matmul(dst, lhsT[0], rhs[1], start=False, stop=False, skip_group_check=again)
                return pe.matmul(dst, lhsT[1], rhs[0], start=False, stop=last, skip_group_check=again)

            def pair(t, *idx):
                return t[0][idx], t[1][idx]

            def project(dst, w, c, act, first, last, again=False):
                for k in range(KC):
                    r = mm3(dst, pair(w, slice(None), k, slice(c * P, (c + 1) * P)), pair(act, slice(None), k),
                            first and k == 0, last and k == KC - 1, again)
                return r

            pe.wait_ge(consts.sem, 3)
            pe.wait_ge(w_in.sem, 16 * N_LOADS)
            pe.wait_ge(prep.sem, PREP_COUNT)
            src = dict(stage, wr=wr_f, wzr=wzr_f, wh=wh_f)
            for i, (dst, name, _, cols) in enumerate(WT):
                if i >= 2:
                    pe.wait_ge(wlo.sem, i - 1)
                t = ST[i % 2]
                if name == "adj":
                    r = pe.transpose(t[:, 0:N], adj_n[:, :], ident[:, :])
                elif name == "qk":
                    for dc in range(KC):
                        for e in range(KC):
                            r = pe.matmul(t[:, dc * D:(dc + 1) * D], stage["Wq"][:, e, dc * P:(dc + 1) * P],
                                          stage["Wk"][:, e, :], start=(e == 0), stop=(e == KC - 1))
                else:
                    for k in range(KC):
                        for o in range(KC):
                            r = pe.transpose(t[:, k * D + o * P:k * D + (o + 1) * P],
                                             src[name][:, o, k * P:(k + 1) * P], ident[:, :])
                r.then_inc(wps.sem, 1)
            pe.wait_ge(wlo.sem, len(WT) + len(WN))

            def nodes_to_features(banks, src_n, done):
                for c in range(KC):
                    for b in range(GB):
                        r = pe.transpose(banks[c][:, b * N:(b + 1) * N], src_n[:, b, c * P:(c + 1) * P], ident[:, :])
                    r.then_inc(done.sem, 1)

            def gru(step, it, g):
                k0 = KC * it
                if step == "init":
                    wait(pe, x_loaded, g, 1)
                    wait(pe, y0, g - 1, 2) if not isinstance(g, int) else None
                    nodes_to_features(SA, x_in, xT_ps)
                if step == "spread":
                    wait(pe, hN_lo, g, k0 + 2)
                    if it == 0:
                        wait(pe, hT0, g, KC)
                    for c in range(KC):
                        for b in range(GB):
                            r = mm3(SA[c][:, b * N:(b + 1) * N], pair(hNs, slice(None), b, slice(c * P, (c + 1) * P)),
                                    (adjT[0][:, :], adjT[1][:, :]), True, True)
                        r.then_inc(a_ps.sem, 1)
                    wait(pe, hT_lo, g, k0 + 2)
                    for c in range(KC):
                        project(SG[c][:, :], UG, c, hTs, True, False)
                if step == "reset":
                    wait(pe, a_lo, g, k0 + 2)
                    for c in range(KC):
                        project(SG[c][:, :], WR, c, aTs, False, True).then_inc(r_ps.sem, 1)
                if step == "update":
                    for c in range(KC):
                        project(SC[c][:, :], WH, c, aTs, True, False)
                    for c in range(KC):
                        wait(pe, r_t, g, k0 + c + 1)
                        project(SG[c][:, :], WZR, c, aTs, False, True, again=True).then_inc(z_ps.sem, 1)
                if step == "candidate":
                    wait(pe, rh_lo, g, k0 + 2)
                    for c in range(KC):
                        project(SC[c][:, :], UH, c, rhs_, False, True).then_inc(c_ps.sem, 1)
                if step == "nodes":
                    wait(pe, h_new, g, k0 + 2)
                    for p in range(2):
                        for b in (0, 1):
                            for c in range(KC):
                                bb = 2 * p + b
                                r = pe.transpose(SA[p][:, b * D + c * P:b * D + (c + 1) * P],
                                                 hT[:, c, bb * N:(bb + 1) * N], ident[:, :])
                        r.then_inc(hN_ps.sem, 1)

            def free_bank(name, k, g):
                i = TILE[name, k]
                if i >= 2:
                    s, n = FREED[PE_TILES[i - 2]]
                    wait(pe, s, g, n)
                else:
                    wait(pe, g3_f, g - 1, GB)

            def tail(step, k, g):
                if (step, k) not in TILE:
                    return
                free_bank(step, k, g)
                t = tile(step, k)
                if step in ("x1T", "x2T", "x3T"):
                    layer = int(step[1]) - 1
                    wait(pe, ln_out, g, GB * (1, 2, 4)[layer])
                    for b in range(GB):
                        r = pe.transpose(t[:, b * N:(b + 1) * N], xs[layer][:, b, k * P:(k + 1) * P], ident[:, :])
                elif step in ("q1T", "q2T", "k2T"):
                    wait(pe, x_lo, g, 2 if step == "q1T" else 4)
                    r = project(t[:, :], dict(q1T=WQK, q2T=WQ2, k2T=WK2)[step], k, xTs, True, True)
                elif step in ("v1", "v2"):
                    w = WV1 if step == "v1" else WV2
                    for b in range(2):
                        bb = 2 * k + b
                        for kk in range(KC):
                            r = mm3(t[:, b * D:(b + 1) * D], pair(xTs, slice(None), kk, slice(bb * N, (bb + 1) * N)),
                                    pair(w, slice(None), kk), kk == 0, kk == KC - 1)
                elif step == "rel":
                    wait(pe, q1_lo, g, 2)
                    for b in range(GB):
                        cols = slice(b * N, (b + 1) * N)
                        for kk in range(KC):
                            r = mm3(t[:, cols], pair(xTs, slice(None), kk, cols), pair(q1s, slice(None), kk, cols),
                                    kk == 0, kk == KC - 1)
                elif step == "out1":
                    wait(pe, v1_lo, g, 2)
                    wait(pe, rm_lo, g, 1)
                    r = mm3(t[:, 0:D + N], pair(vr, slice(None), k, slice(D, D + N)), pair(vr, slice(None), k), True, True)
                elif step == "score":
                    b, half_ = k // 2, k % 2
                    wait(pe, stacked, g, 6 * HC)
                    for j in range(HC):
                        hh = half_ * HC + j
                        cols = slice(b * N, (b + 1) * N)
                        r = pe.matmul(t[:, j * N:(j + 1) * N], qst[:, hh, cols], kst[:, hh, cols], start=True, stop=True)
                elif step == "probT":
                    wait(pe, ex_f, g, k + 1)
                    for j in range(HC):
                        r = pe.transpose(t[:, j * N:(j + 1) * N], ex[:, k % 4, j * N:(j + 1) * N], ident[:, :])
                elif step == "head_out":
                    wait(pe, pT_lo, g, 2 * k + 2)
                    wait(pe, v2_lo, g, 2)
                    for hh in range(H):
                        r = mm3(t[:, hh * HD:(hh + 1) * HD], pair(pTs, slice(None), k % 2, hh),
                                pair(v2s, slice(None), k, slice(hh * HD, (hh + 1) * HD)), True, True)
                elif step == "oT":
                    wait(pe, o_f, g, GB)
                    for b in range(GB):
                        r = pe.transpose(t[:, b * N:(b + 1) * N], o_n[:, b, k * P:(k + 1) * P], ident[:, :])
                elif step == "proj":
                    wait(pe, oT_lo, g, 2)
                    for b in range(2):
                        bb = 2 * k + b
                        for kk in range(KC):
                            r = mm3(t[:, b * D:(b + 1) * D], pair(oTs, slice(None), kk, slice(bb * N, (bb + 1) * N)),
                                    pair(WP2, slice(None), kk), kk == 0, kk == KC - 1)
                elif step == "h3":
                    wait(pe, x_lo, g, 6)
                    for kk in range(KC):
                        r = mm3(t[:, 0:D + 2], pair(xTs, slice(None), kk, slice(k * N, (k + 1) * N)),
                                pair(WG, slice(None), kk), kk == 0, kk == KC - 1)
                elif step == "edge":
                    wait(pe, h3_f, g, GB)
                    for b in range(GB):
                        r = pe.transpose(t[:, b * N:(b + 1) * N],
                                         h3f[:, b, D + 1:D + 2].broadcast_to([P, P]), ident[:, :])
                elif step == "attT":
                    wait(pe, eex_f, g, 1)
                    for b in range(GB):
                        r = pe.transpose(t[:, b * N:(b + 1) * N], eex[:, b * N:(b + 1) * N], ident[:, :])
                elif step == "out3":
                    wait(pe, a3_lo, g, 1)
                    wait(pe, h3_lo, g, 1)
                    for b in range(2):
                        bb = 2 * k + b
                        r = mm3(t[:, b * D:(b + 1) * D], pair(aT3, slice(None), bb), pair(h3s, slice(None), bb), True, True)
                r.then_inc(tile_ps.sem, 1)

            run_all(pe, gru, tail)

        @block.scalar
        def _(act):
            def scaled(dst, src_, scale, done):
                act.activation(dst, src_, ACT.Copy, scale=scale).then_inc(done.sem, 1)

            for i, (dst, _, scale, cols) in enumerate(WT):
                act.wait_ge(wps.sem, i + 1)
                if cols == N:
                    scaled(dst[0][:, :], ST[i % 2][:, 0:N], scale, whi)
                else:
                    scaled(dst[0][:, :, :], ST[i % 2][:, :].rearrange("p (k d) -> p k d", k=KC), scale, whi)
            act.wait_ge(w_in.sem, 16 * N_LOADS)
            act.wait_ge(prep.sem, PREP_COUNT)
            for dst, src_, scale in WN:
                scaled(dst[0][:, :, :], src_[:, :, :], scale, whi)
            act.wait_ge(wlo.sem, len(WT) + len(WN))

            def gru(step, it, g):
                k0 = KC * it
                if step == "init":
                    for c in range(KC):
                        wait(act, xT_ps, g, c + 1)
                        act.activation(hT[:, c, :], SA[c][:, :], ACT.Copy).then_inc(hT0.sem, 1)
                    for p in range(2):
                        wait(act, x_loaded, g, 1)
                        act.activation(hNs[0][:, 2 * p:2 * p + 2, :], x_in[:, 2 * p:2 * p + 2, :], ACT.Copy)\
                            .then_inc(hN_hi.sem, 1)
                    for c in range(KC):
                        wait(act, hT0, g, c + 1)
                        act.activation(hTs[0][:, c, :], hT[:, c, :], ACT.Copy).then_inc(hT_hi.sem, 1)
                    act.activation(x_keep[:, :, :], x_in[:, :, :], ACT.Copy).then_inc(x_freed.sem, 1)
                if step == "spread":
                    for c in range(KC):
                        wait(act, a_ps, g, k0 + c + 1)
                        scaled(aTs[0][:, c, :], SA[c][:, :], 1 / ADJ_SCALE, a_hi)
                if step == "reset":
                    for c in range(KC):
                        wait(act, r_ps, g, k0 + c + 1)
                        act.activation(t_reset[:, c, :], SG[c][:, :], ACT.Tanh, bias=gru_bias[:, 0, c:c + 1],
                                       scale=0.5 / W_SCALE).then_inc(r_t.sem, 1)
                if step == "update":
                    for c in range(KC):
                        wait(act, z_ps, g, k0 + c + 1)
                        act.activation(t_update[:, c, :], SG[c][:, :], ACT.Tanh, bias=gru_bias[:, 1, c:c + 1],
                                       scale=0.5 / W_SCALE).then_inc(z_t.sem, 1)
                if step == "candidate":
                    for c in range(KC):
                        wait(act, c_ps, g, k0 + c + 1)
                        act.activation(cand[:, c, :], SC[c][:, :], ACT.Tanh, bias=gru_bias[:, 2, c:c + 1],
                                       scale=1 / W_SCALE).then_inc(c_t.sem, 1)
                if step == "state" and it + 1 < ITERS:
                    for c in range(KC):
                        wait(act, h_new, g, k0 + c + 1)
                        act.activation(hTs[0][:, c, :], hT[:, c, :], ACT.Copy).then_inc(hT_hi.sem, 1)
                if step == "nodes" and it + 1 < ITERS:
                    for p in range(2):
                        wait(act, hN_ps, g, k0 + p + 1)
                        act.activation(hNs[0][:, 2 * p:2 * p + 2, :], SA[p][:, :].rearrange("p (b d) -> p b d", b=2),
                                       ACT.Copy).then_inc(hN_hi.sem, 1)

            def tail(step, k, g):
                if (step, k) in TILE:
                    tile_full(act, g, step, k)
                    t = tile(step, k)
                pairs = slice(2 * k, 2 * k + 2)
                if step in ("x1T", "x2T", "x3T"):
                    scaled(xTs[0][:, k, :], t[:, :], 1.0, x_hi)
                elif step == "q1T":
                    scaled(q1s[0][:, k, :], t[:, :], 1 / W_SCALE, q1_hi)
                elif step == "v1":
                    scaled(vr[0][:, pairs, 0:D], t[:, :].rearrange("p (b d) -> p b d", b=2), 1 / W_SCALE, v1_hi)
                elif step == "rel":
                    wait(act, rm_f, g, 1)
                    scaled(vr[0][:, :, D:D + N], rm[:, :].rearrange("p (b n) -> p b n", b=GB), 1.0, rm_hi)
                elif step == "out1":
                    act.activation(u1[:, k, :], t[:, 0:D], ACT.Copy).then_inc(u1_f.sem, 1)
                elif step == "q2T":
                    scaled(q2s[0][:, k, :], t[:, :], 1 / W_SCALE, q2_hi)
                elif step == "k2T":
                    scaled(k2s[0][:, k, :], t[:, :], 1 / W_SCALE, k2_hi)
                elif step == "v2":
                    scaled(v2s[0][:, pairs, :], t[:, :].rearrange("p (b d) -> p b d", b=2), 1 / W_SCALE, v2_hi)
                elif step == "score":
                    wait(act, nmax_f, g, k + 1)
                    for j in range(HC):
                        r = act.activation(ex[:, k % 4, j * N:(j + 1) * N], sm[:, k % 2, j * N:(j + 1) * N], ACT.Exp,
                                           bias=nmax[:, k, j:j + 1], accum_out=rsum[:, k, j:j + 1])
                    r.then_inc(ex_f.sem, 1)
                elif step == "probT":
                    b, half_ = k // 2, k % 2
                    scaled(pTs[0][:, b % 2, half_ * HC:(half_ + 1) * HC, :],
                           t[:, :].rearrange("p (h n) -> p h n", h=HC), 1.0, pT_hi)
                elif step == "oT":
                    scaled(oTs[0][:, k, :], t[:, :], 1.0, oT_hi)
                elif step == "h3":
                    scaled(h3f[:, k, :], t[:, 0:D + 2], 1 / W_SCALE, h3_f)
                elif step == "edge":
                    wait(act, h3_f, g, GB)
                    for b in range(GB):
                        r = act.activation(presum[:, b * N:(b + 1) * N], t[:, b * N:(b + 1) * N], ACT.Identity,
                                           bias=h3f[:, b, D:D + 1])
                    r.then_inc(presum_f.sem, 1)
                elif step == "edge_soft":
                    wait(act, enmax_f, g, 1)
                    for b in range(GB):
                        r = act.activation(eex[:, b * N:(b + 1) * N], edge[:, b * N:(b + 1) * N], ACT.Exp,
                                           bias=enmax[:, b:b + 1], accum_out=ersum[:, b:b + 1])
                    r.then_inc(eex_f.sem, 1)
                elif step == "attT":
                    scaled(aT3[0][:, :, :], t[:, :].rearrange("p (b n) -> p b n", b=GB), 1.0, a3_hi)
                elif step == "elu":
                    wait(act, m3_f, g, 1)
                    act.activation(e3[:, :, :], m3[:, :, :], ACT.Exp).then_inc(e3_f.sem, 1)

            run_all(act, gru, tail)

        @block.vector
        def _(dve):
            def low(dst, src_, scale, hi, done):
                dve.scalar_tensor_tensor(out=dst, in0=src_, scalar=scale, in1=hi, op0=ALU.mult, op1=ALU.subtract)\
                    .then_inc(done.sem, 1)

            g3_f.setup(dve)
            dve.wait_ge(w_in.sem, 16 * N_LOADS)
            count = 0

            def prepared(ins):
                nonlocal count
                count += 1
                ins.then_inc(prep.sem, 1)
                return count

            w3f, w4f, w5f = stage["w3"], stage["w4"], stage["w5"]
            prepared(dve.tensor_tensor(wr_f, w4f[:, :, 0:D], w4f[:, :, D:2 * D], ALU.add))
            n = prepared(dve.tensor_tensor(wzr_f, w3f[:, :, 0:D], w3f[:, :, D:2 * D], ALU.add))
            prepared(dve.tensor_tensor(wh_f, w5f[:, :, 0:D], w5f[:, :, D:2 * D], ALU.add))
            dve.wait_ge(prep.sem, n)
            prepared(dve.tensor_tensor(wzr_f, wzr_f, wr_f, ALU.subtract))
            prepared(dve.tensor_scalar(no_edge[:, :], adj_n[:, :], 0.0, NO_EDGE, ALU.is_equal, ALU.mult))
            prepared(dve.tensor_tensor(gru_bias[:, 0, :], bias_in[:, 2, :], bias_in[:, 1, :], ALU.add))
            prepared(dve.tensor_tensor(gru_bias[:, 1, :], bias_in[:, 0, :], bias_in[:, 1, :], ALU.add))
            prepared(dve.tensor_tensor(gru_bias[:, 2, :], bias_in[:, 3, :], bias_in[:, 4, :], ALU.add))
            dve.wait_ge(prep.sem, count)
            prepared(dve.tensor_scalar(gru_bias[:, 0:2, :], gru_bias[:, 0:2, :], 0.5, None, ALU.mult))
            for i in range(2):
                prepared(dve.tensor_tensor(wa_t[:, 2 * i:2 * i + 2, :], stage["wg"],
                                           a_bc[:, i:i + 1, :].broadcast_to([P, KC, D]), ALU.mult))
                dve.wait_ge(prep.sem, count)
                prepared(dve.tensor_reduce(out=wa_f[:, :, i:i + 1], in_=wa_t[:, 2 * i:2 * i + 2, :], op=ALU.add, axis=AX.X))
            assert count == PREP_COUNT
            dve.wait_ge(prep.sem, count)
            for i, (dst, _, scale, cols) in enumerate(WT):
                dve.wait_ge(whi.sem, i + 1)
                if cols == N:
                    low(dst[1][:, :], ST[i % 2][:, 0:N], scale, dst[0][:, :], wlo)
                else:
                    low(dst[1][:, :, :], ST[i % 2][:, :].rearrange("p (k d) -> p k d", k=KC), scale, dst[0][:, :, :], wlo)
            for i, (dst, src_, scale) in enumerate(WN):
                dve.wait_ge(whi.sem, len(WT) + i + 1)
                low(dst[1][:, :, :], src_[:, :, :], scale, dst[0][:, :, :], wlo)
            dve.wait_ge(wlo.sem, len(WT) + len(WN))

            def gru(step, it, g):
                k0 = KC * it
                if step == "init":
                    for p in range(2):
                        ps = slice(2 * p, 2 * p + 2)
                        wait(dve, hN_hi, g, p + 1)
                        dve.tensor_tensor(hNs[1][:, ps, :], x_in[:, ps, :], hNs[0][:, ps, :], ALU.subtract)\
                            .then_inc(hN_lo.sem, 1)
                if step == "spread":
                    for c in range(KC):
                        wait(dve, a_hi, g, k0 + c + 1)
                        low(aTs[1][:, c, :], SA[c][:, :], 1 / ADJ_SCALE, aTs[0][:, c, :], a_lo)
                if step == "reset":
                    for c in range(KC):
                        wait(dve, r_t, g, k0 + c + 1)
                        dve.scalar_tensor_tensor(out=rh2[:, c, :], in0=t_reset[:, c, :], scalar=1.0, in1=hT[:, c, :],
                                                 op0=ALU.add, op1=ALU.mult).then_inc(rh_f.sem, 1)
                        wait(dve, rh_f, g, k0 + c + 1)
                        dve.tensor_copy(rhs_[0][:, c, :], rh2[:, c, :]).then_inc(rh_hi.sem, 1)
                        wait(dve, rh_hi, g, k0 + c + 1)
                        dve.tensor_tensor(rhs_[1][:, c, :], rh2[:, c, :], rhs_[0][:, c, :], ALU.subtract)\
                            .then_inc(rh_lo.sem, 1)
                if step == "candidate":
                    for c in range(KC):
                        wait(dve, d_f, g, k0 + c + 1)
                        wait(dve, z_t, g, k0 + c + 1)
                        dve.scalar_tensor_tensor(out=step_[:, c, :], in0=t_update[:, c, :], scalar=1.0,
                                                 in1=diff[:, c, :], op0=ALU.add, op1=ALU.mult).then_inc(u_f.sem, 1)
                        wait(dve, u_f, g, k0 + c + 1)
                        dve.scalar_tensor_tensor(out=hT[:, c, :], in0=step_[:, c, :], scalar=0.5, in1=hT[:, c, :],
                                                 op0=ALU.mult, op1=ALU.add).then_inc(h_new.sem, 1)
                if step == "nodes":
                    for p in range(2):
                        ps = slice(2 * p, 2 * p + 2)
                        t = SA[p][:, :].rearrange("p (b d) -> p b d", b=2)
                        if it + 1 < ITERS:
                            wait(dve, hN_hi, g, k0 + 2 + p + 1)
                            dve.tensor_tensor(hNs[1][:, ps, :], t, hNs[0][:, ps, :], ALU.subtract)\
                                .then_inc(hN_lo.sem, 1)
                        else:
                            wait(dve, x_freed, g, 1)
                            wait(dve, hN_ps, g, k0 + p + 1)
                            dve.tensor_tensor(gru_out[:, ps, :], t, x_keep[:, ps, :], ALU.add).then_inc(y0.sem, 1)

            def layer_norm(u, g, src_, dst):
                for b in range(GB):
                    dve.bn_stats(out=stats[:, u, b, :], in_=src_[:, b, :]).then_inc(ln_stats.sem, 1)
                gate(dve, ln_stats, g, GB * u + GB)
                for b in range(GB):
                    dve.bn_aggr(out=meanvar[:, u, b, :], in_=stats[:, u, b, :]).then_inc(ln_aggr.sem, 1)
                wait(dve, ln_aggr, g, GB * u + GB)
                dve.tensor_scalar(vareps[:, u, :], meanvar[:, u, :, 1], EPS, None, ALU.add).then_inc(ln_ve.sem, 1)
                wait(dve, ln_rstd, g, u + 1)
                for b in range(GB):
                    dve.tensor_scalar(dst[:, b, :], src_[:, b, :], meanvar[:, u, b, 0:1], rstd[:, u, b:b + 1],
                                      ALU.subtract, ALU.mult).then_inc(ln_out.sem, 1)

            def tail(step, k, g):
                t = tile(step, k) if (step, k) in TILE else None
                pairs = slice(2 * k, 2 * k + 2)
                if step == "ln":
                    if k == 0:
                        wait(dve, y0, g, 2)
                        layer_norm(0, g, gru_out, xs[0])
                    elif k == 1:
                        wait(dve, y1_f, g, GB)
                        layer_norm(1, g, y, xs[1])
                    elif k == 2:
                        wait(dve, proj_f, g, 2)
                        layer_norm(2, g, proj_o, ln_o)
                    elif k == 3:
                        wait(dve, y2_f, g, 1)
                        layer_norm(3, g, y, xs[2])
                    else:
                        wait(dve, y3_f, g, 1)
                        wait(dve, stored, g - 1, 1)
                        layer_norm(4, g, y, xs[3])
                elif step in ("x1T", "x2T", "x3T"):
                    wait(dve, x_hi, g, 2 * (int(step[1]) - 1) + k + 1)
                    low(xTs[1][:, k, :], t[:, :], 1.0, xTs[0][:, k, :], x_lo)
                elif step == "q1T":
                    wait(dve, q1_hi, g, k + 1)
                    low(q1s[1][:, k, :], t[:, :], 1 / W_SCALE, q1s[0][:, k, :], q1_lo)
                elif step == "v1":
                    wait(dve, v1_hi, g, k + 1)
                    low(vr[1][:, pairs, 0:D], t[:, :].rearrange("p (b d) -> p b d", b=2), 1 / W_SCALE,
                        vr[0][:, pairs, 0:D], v1_lo)
                elif step == "rel":
                    tile_full(dve, g, step, k)
                    rmv = rm[:, :].rearrange("p (b n) -> p b n", b=GB)
                    ab = adj_n[:, :].rearrange("p (a n) -> p a n", a=1).broadcast_to([P, GB, N])
                    dve.tensor_tensor(rmv, t[:, :].rearrange("p (b n) -> p b n", b=GB), ab, ALU.mult)\
                        .then_inc(rm_f.sem, 1)
                    wait(dve, rm_hi, g, 1)
                    dve.tensor_tensor(vr[1][:, :, D:D + N], rmv, vr[0][:, :, D:D + N], ALU.subtract)\
                        .then_inc(rm_lo.sem, 1)
                elif step == "out1":
                    wait(dve, u1_f, g, k + 1)
                    if k:
                        wait(dve, n2_f, g, k)
                    dve.scalar_tensor_tensor(out=junk[:, :], in0=t[:, D:D + N], scalar=1.0, in1=ident[:, :],
                                             op0=ALU.mult, op1=ALU.mult, accum_out=norm2[:, k:k + 1])\
                        .then_inc(n2_f.sem, 1)
                elif step == "mix1":
                    wait(dve, rn_f, g, 1)
                    for b in range(GB):
                        dve.scalar_tensor_tensor(out=y[:, b, :], in0=u1[:, b, :], scalar=rstd[:, 5, b:b + 1],
                                                 in1=xs[0][:, b, :], op0=ALU.mult, op1=ALU.add).then_inc(y1_f.sem, 1)
                elif step == "q2T":
                    wait(dve, q2_hi, g, k + 1)
                    low(q2s[1][:, k, :], t[:, :], 1 / W_SCALE, q2s[0][:, k, :], q2_lo)
                elif step == "k2T":
                    wait(dve, k2_hi, g, k + 1)
                    low(k2s[1][:, k, :], t[:, :], 1 / W_SCALE, k2s[0][:, k, :], k2_lo)
                elif step == "v2":
                    wait(dve, v2_hi, g, k + 1)
                    low(v2s[1][:, pairs, :], t[:, :].rearrange("p (b d) -> p b d", b=2), 1 / W_SCALE,
                        v2s[0][:, pairs, :], v2_lo)
                elif step == "score":
                    tile_full(dve, g, step, k)
                    if k >= 2:
                        wait(dve, ex_f, g, k - 1)
                    smv = sm[:, k % 2, :].rearrange("p (h m) -> p h m", h=HC)
                    mb = no_edge[:, :].rearrange("p (a m) -> p a m", a=1).broadcast_to([P, HC, N])
                    dve.tensor_tensor(smv, t[:, :].rearrange("p (h m) -> p h m", h=HC), mb, ALU.add)\
                        .then_inc(sm_f.sem, 1)
                    wait(dve, sm_f, g, k + 1)
                    dve.tensor_reduce(out=nmax[:, k, :], in_=smv, op=ALU.max, axis=AX.X, negate=True)\
                        .then_inc(nmax_f.sem, 1)
                elif step == "probT":
                    b, half_ = k // 2, k % 2
                    wait(dve, pT_hi, g, k + 1)
                    hs = slice(half_ * HC, (half_ + 1) * HC)
                    low(pTs[1][:, b % 2, hs, :], t[:, :].rearrange("p (h n) -> p h n", h=HC), 1.0,
                        pTs[0][:, b % 2, hs, :], pT_lo)
                elif step == "head_out":
                    wait(dve, ex_f, g, 2 * k + 2)
                    dve.reciprocal(rinv[:, 2 * k:2 * k + 2, :], rsum[:, 2 * k:2 * k + 2, :]).then_inc(rinv_f.sem, 1)
                    wait(dve, rinv_f, g, k + 1)
                    tile_full(dve, g, step, k)
                    ri = rinv[:, 2 * k:2 * k + 2, :].rearrange("p a (h o) -> p (a h) o", o=1).broadcast_to([P, H, HD])
                    dve.tensor_tensor(o_n[:, k, :].rearrange("p (h d) -> p h d", h=H),
                                      t[:, 0:D].rearrange("p (h d) -> p h d", h=H), ri, ALU.mult).then_inc(o_f.sem, 1)
                elif step == "oT":
                    wait(dve, oT_hi, g, k + 1)
                    low(oTs[1][:, k, :], t[:, :], 1.0, oTs[0][:, k, :], oT_lo)
                elif step == "proj":
                    tile_full(dve, g, step, k)
                    bb = bproj_b[:, :].rearrange("p (a d) -> p a d", a=1).broadcast_to([P, 2, D])
                    dve.scalar_tensor_tensor(out=proj_o[:, pairs, :], in0=t[:, :].rearrange("p (b d) -> p b d", b=2),
                                             scalar=1 / W_SCALE, in1=bb, op0=ALU.mult, op1=ALU.add)\
                        .then_inc(proj_f.sem, 1)
                elif step == "mix2":
                    wait(dve, ln_out, g, 12)
                    gb = gamma_b[:, :].rearrange("p (a d) -> p a d", a=1).broadcast_to([P, GB, D])
                    dve.tensor_tensor(ln_g[:, :, :], ln_o[:, :, :], gb, ALU.mult).then_inc(lng_f.sem, 1)
                    wait(dve, lng_f, g, 1)
                    wait(dve, baseo_f, g, 1)
                    dve.tensor_tensor(y[:, :, :], ln_g[:, :, :], base2[:, :, :], ALU.add).then_inc(y2_f.sem, 1)
                elif step == "edge":
                    wait(dve, h3_f, g, GB)
                    dve.tensor_copy(h3s[0][:, :, :], h3f[:, :, 0:D]).then_inc(h3_hi.sem, 1)
                    wait(dve, h3_hi, g, 1)
                    dve.tensor_tensor(h3s[1][:, :, :], h3f[:, :, 0:D], h3s[0][:, :, :], ALU.subtract)\
                        .then_inc(h3_lo.sem, 1)
                elif step == "edge_soft":
                    wait(dve, presum_f, g, 1)
                    ev = edge[:, :].rearrange("p (b m) -> p b m", b=GB)
                    ab = adj_n[:, :].rearrange("p (a n) -> p a n", a=1).broadcast_to([P, GB, N])
                    dve.scalar_tensor_tensor(out=edge[:, :], in0=presum[:, :], scalar=SLOPE, in1=presum[:, :],
                                             op0=ALU.mult, op1=ALU.max).then_inc(edge_f.sem, 1)
                    wait(dve, edge_f, g, 1)
                    dve.tensor_tensor(ev, ev, ab, ALU.mult).then_inc(edge_f.sem, 1)
                    wait(dve, edge_f, g, 2)
                    dve.tensor_reduce(out=enmax[:, :], in_=ev, op=ALU.max, axis=AX.X, negate=True)\
                        .then_inc(enmax_f.sem, 1)
                elif step == "attT":
                    wait(dve, eex_f, g, 1)
                    dve.reciprocal(erinv[:, :], ersum[:, :]).then_inc(erinv_f.sem, 1)
                    wait(dve, a3_hi, g, 1)
                    low(aT3[1][:, :, :], t[:, :].rearrange("p (b n) -> p b n", b=GB), 1.0, aT3[0][:, :, :], a3_lo)
                elif step == "out3":
                    tile_full(dve, g, step, k)
                    wait(dve, erinv_f, g, 1)
                    wait(dve, bh_f, g, 1)
                    for b in range(2):
                        bb = 2 * k + b
                        dve.scalar_tensor_tensor(out=g3[:, bb, :], in0=t[:, b * D:(b + 1) * D],
                                                 scalar=erinv[:, bb:bb + 1], in1=bh[:, bb, :],
                                                 op0=ALU.mult, op1=ALU.add).then_inc(g3_f.sem, 1)
                elif step == "elu":
                    wait(dve, g3_f, g, GB)
                    dve.tensor_scalar(m3[:, :, :], g3[:, :, :], 0.0, None, ALU.min).then_inc(m3_f.sem, 1)
                    dve.scalar_tensor_tensor(out=g3[:, :, :], in0=g3[:, :, :], scalar=0.0, in1=xs[2][:, :, :],
                                             op0=ALU.max, op1=ALU.add).then_inc(p3_f.sem, 1)
                    wait(dve, p3_f, g, 1)
                    wait(dve, e3_f, g, 1)
                    dve.scalar_tensor_tensor(out=y[:, :, :], in0=e3[:, :, :], scalar=-1.0, in1=g3[:, :, :],
                                             op0=ALU.add, op1=ALU.add).then_inc(y3_f.sem, 1)

            run_all(dve, gru, tail)


_INS = ['x', 'adj', 'L0_gnn_w3_w', 'L0_gnn_w3_b', 'L0_gnn_u3_w', 'L0_gnn_u3_b', 'L0_gnn_w4_w', 'L0_gnn_w4_b',
        'L0_gnn_w5_w', 'L0_gnn_w5_b', 'L0_gnn_u5_w', 'L0_gnn_u5_b', 'L1_gnn_Wq', 'L1_gnn_Wk', 'L1_gnn_Wv',
        'L2_gnn_w_qkv', 'L2_gnn_w_proj', 'L2_gnn_b_proj', 'L2_gnn_ln_gamma', 'L2_gnn_ln_beta',
        'L3_gnn_W', 'L3_gnn_a', 'L3_gnn_beta']


def kernel(**inputs):
    import numpy as _np
    import concourse.bacc as _bacc
    from concourse import mybir as _mybir
    from concourse.bass_utils import run_bass_kernel_spmd as _run

    nc = _bacc.Bacc("TRN2", target_bir_lowering=False, num_devices=1)
    arrays, args = {}, []
    for name in _INS:
        a = _np.ascontiguousarray(inputs[name])
        arrays[f"in_{name}"] = a
        args.append(nc.dram_tensor(f"in_{name}", a.shape, _mybir.dt.from_np(a.dtype), kind="ExternalInput").ap())
    args.append(nc.dram_tensor("out_x", (B, N, D), F32, kind="ExternalOutput").ap())
    build(nc, *args)
    r = _run(nc, [arrays], core_ids=[0])
    return r.results[0]["out_x"]
```

```python
import concourse.bass as bass
from concourse import mybir
from contextlib import ExitStack

F32 = mybir.dt.float32
F16 = mybir.dt.float16
ALU = mybir.AluOpType
ACT = mybir.ActivationFunctionType
AX = mybir.AxisListType

B, N, D, H = 64, 128, 256, 8
P = 128
GB = 4
NG = B // GB
T = GB * N
KC = D // P
HD = D // H
HC = P // HD
ITERS = 3
EPS = 1e-5
W_SCALE = 16.0
ADJ_SCALE = 64.0
NO_EDGE = -1e30
SLOPE = 0.2

GRU_STEPS = ("spread", "keep", "reset", "gated", "fresh", "update", "candidate", "blend", "state", "nodes")


def gru_steps(more):
    out = []
    for it in range(ITERS):
        for s in GRU_STEPS:
            out.append(("gru", s, it))
            if s == "fresh" and it == 0:
                out.append(("gru", "x_keep", it))
            if s == "candidate" and it == ITERS - 1 and more:
                out.append(("gru", "next_x", it))
    return out


def att_steps():
    t = [("ln", 0), ("ln_out", 0), ("x1T", 0), ("x1T", 1), ("q1T", 0), ("q1T", 1), ("v1", 0), ("v1", 1), ("rel", 0)]
    t += [("out1", b) for b in range(GB)] + [("mix1", 0), ("ln", 1), ("ln_out", 1)]
    t += [("x2T", 0), ("x2T", 1), ("q2T", 0), ("q2T", 1), ("k2T", 0), ("k2T", 1), ("v2", 0), ("v2", 1)]
    t += [("score", 0), ("score", 1), ("score", 2), ("score", 3)]
    for b in range(GB):
        t += [("probT", 2 * b), ("probT", 2 * b + 1), ("head_out", b)]
        if b + 2 < GB:
            t += [("score", 2 * b + 4), ("score", 2 * b + 5)]
    t += [("oT", 0), ("oT", 1), ("proj", 0), ("proj", 1)]
    return [("att",) + s for s in t]


def end_steps():
    t = [("ln", 2), ("ln_out", 2), ("mix2", 0), ("ln", 3), ("ln_out", 3), ("x3T", 0), ("x3T", 1)]
    t += [("h3", b) for b in range(GB)]
    t += [("edge", 0), ("edge_soft", 0), ("attT", 0), ("out3", 0), ("out3", 1), ("elu", 0), ("ln", 4), ("ln_out", 4)]
    return [("end",) + s for s in t]


NO_TILE = ("ln", "ln_out", "mix1", "mix2", "edge_soft", "elu")
ATT_TILES = [s[1:] for s in att_steps() if s[1] not in NO_TILE]
END_TILES = [s[1:] for s in end_steps() if s[1] not in NO_TILE]

MERGE = {
    "pe": "aaggaageaaeagaeeageaagaaageaeageeagageegaaaaeagaeagaeaggagaagggeaa"
          "ggeaegaaggaagagaagaaaegaaagggagea",
    "dve": "agaggeaaegaaaaaegggeaaaageaaeeeeeaggaagaaaeeaeaagggaaaagggegaaggea"
           "gaeagggeaaaaagaaggaeaagaeagagagga",
    "act": "eaeegagaaegaaaaaaaagaaeagaggeegeeaaggegaeaaaeagageeaaggaeaeaagggga"
           "gggaeaaagagggaaaaaaaagegaaaaggegg",
    "pool": "aaaeggeaaeaaaaaaeaageeaggagaeeeggaaggageaaageaaaggegggaeaaaegaaaaa"
            "aagaggeeeagaggggegeggaaaaaaaaaggg",
}


def body_order(engine, streams):
    steps = {"g": gru_steps(True), "a": att_steps(), "e": end_steps()}
    out = [steps[c].pop(0) for c in MERGE[engine]]
    assert not any(steps.values())
    return [s for s in out if s[0] in streams]


class Signal:

    def __init__(self, ctx, nc, name, per_group, step=1, base=0):
        self.sem = ctx.enter_context(nc.semaphore(name))
        self.per_group, self.step = per_group, step
        self.base = base

    def setup(self, eng):
        eng.sem_inc(self.sem, self.base)

    def at(self, g, k):
        return (g * self.per_group + k) * self.step + self.base


def build(nc, x, adj, w3_w, w3_b, u3_w, u3_b, w4_w, w4_b, w5_w, w5_b, u5_w, u5_b, Wq, Wk, Wv,
          w_qkv, w_proj, b_proj, ln_gamma, ln_beta, W3l, a3l, beta3l, out):
    ctx = ExitStack()
    with ctx:
        def sb(name, shape, dt=F32):
            return ctx.enter_context(nc.sbuf_tensor(name, shape, dt))

        def hilo(name, shape):
            return sb(name + "_hi", shape, F16), sb(name + "_lo", shape, F16)

        def sig(name, per_group, step=1, base=0):
            return Signal(ctx, nc, name, per_group, step, base)

        ident = sb("ident", [P, P])
        adj_n = sb("adj_n", [P, N])
        no_edge = sb("no_edge", [P, N])
        half = sb("half", [P, 6 * GB])
        gru_bias = sb("gru_bias", [P, 3, KC])
        bproj_b = sb("bproj_b", [P, D])
        gamma_b = sb("gamma_b", [P, D])
        lnbeta_b = sb("lnbeta_b", [P, D])
        beta_b = sb("beta_b", [P, 1])
        adjT = hilo("adjT", [P, N])
        WR, WZR, WH = hilo("WR", [P, KC, D]), hilo("WZR", [P, KC, D]), hilo("WH", [P, KC, D])
        UG, UH = hilo("UG", [P, KC, D]), hilo("UH", [P, KC, D])
        WQK, WV1 = hilo("WQK", [P, KC, D]), hilo("WV1", [P, KC, D])
        WQ2, WK2, WV2 = hilo("WQ2", [P, KC, D]), hilo("WK2", [P, KC, D]), hilo("WV2", [P, KC, D])
        WP2, WG = hilo("WP2", [P, KC, D]), hilo("WG", [P, KC, D + 2])

        x_in = sb("x_in", [P, GB, D])
        x_keep = sb("x_keep", [P, GB, D])
        hT = sb("hT", [P, KC, T])
        xT = sb("xT", [P, KC, T])
        hTs, hNs = hilo("hTs", [P, KC, T]), hilo("hNs", [P, GB, D])
        aTs, rhs_ = hilo("aTs", [P, KC, T]), hilo("rhTs", [P, KC, T])
        t_reset, t_update = sb("t_reset", [P, KC, T]), sb("t_update", [P, KC, T])
        cand, rh2 = sb("cand", [P, KC, T]), sb("rh2", [P, KC, T])
        diff = sb("diff", [P, KC, T])
        gru_out = rh2[:, :, :].rearrange("p c t -> p (c t)").rearrange("p (b d) -> p b d", b=GB)
        y = sb("y", [P, GB, D])
        y_end = sb("y_end", [P, GB, D])
        xs = [sb("x1", [P, GB, D]), sb("x2", [P, GB, D]), sb("x3", [P, GB, D]), y_end]
        xTs, x3Ts = hilo("xTs", [P, KC, T]), hilo("x3Ts", [P, KC, T])
        q1s = hilo("q1s", [P, KC, T])
        vr = hilo("vr", [P, GB, D + N])
        rm = sb("rm", [P, T])
        u1 = sb("u1", [P, GB, D])
        junk = sb("junk", [P, N])
        norm2 = sb("norm2", [P, GB])
        q2s, k2s = hilo("q2s", [P, KC, T]), hilo("k2s", [P, KC, T])
        v2s = hilo("v2s", [P, GB, D])
        qst, kst = sb("qst", [3 * HD, H, T], F16), sb("kst", [3 * HD, H, T], F16)
        sm = sb("sm", [P, 2, HC * N])
        nmax = sb("nmax", [P, 2 * GB, HC])
        rsum = sb("rsum", [P, 2 * GB, HC])
        rinv = sb("rinv", [P, 2 * GB, HC])
        ex = sb("ex", [P, 4, HC * N])
        pTs = hilo("pTs", [P, 2, H, N])
        o_n = sb("o_n", [P, GB, D])
        oTs = q1s
        proj_o = sb("proj_o", [P, GB, D])
        base2 = sb("base2", [P, GB, D])
        ln_o = sb("ln_o", [P, GB, D])
        ln_g = sb("ln_g", [P, GB, D])
        h3f = sb("h3f", [P, GB, D + 2])
        h3s = hilo("h3s", [P, GB, D])
        flat_o = ln_o[:, :, :].rearrange("p b d -> p (b d)")
        presum, edge = flat_o[:, 0:T], flat_o[:, T:2 * T]
        enmax, ersum, erinv = sb("enmax", [P, GB]), sb("ersum", [P, GB]), sb("erinv", [P, GB])
        eex = ln_g[:, :, :].rearrange("p b d -> p (b d)")[:, 0:T]
        aT3 = hilo("aT3", [P, GB, N])
        bh = base2
        g3, m3, e3 = y_end, ln_g, ln_o
        stats = sb("stats", [P, 5, GB, 6])
        meanvar = sb("meanvar", [P, 5, GB, 2])
        vareps, rstd = sb("vareps", [P, 6, GB]), sb("rstd", [P, 6, GB])

        def bank(name):
            return ctx.enter_context(nc.psum_tensor(name, [P, 512], F32))
        SA = [bank(f"SA{i}") for i in range(2)]
        SG = [bank(f"SG{i}") for i in range(2)]
        ST = [bank(f"ST{i}") for i in range(2)]
        SE = [bank(f"SE{i}") for i in range(2)]

        w_in, consts = sig("w_in", 0, 16), sig("consts", 0)
        prep, wps, whi, wlo = sig("prep", 0), sig("wps", 0), sig("whi", 0), sig("wlo", 0)
        x_loaded = sig("x_loaded", 1, 16)
        x_kept = sig("x_kept", 1)
        xT_ps, hT0 = sig("xT_ps", KC), sig("hT0", KC)
        hT_hi, hT_lo = sig("hT_hi", KC * ITERS), sig("hT_lo", KC * ITERS)
        hN_hi, hN_lo = sig("hN_hi", 2 * ITERS), sig("hN_lo", 2 * ITERS)
        a_ps, a_hi, a_lo = sig("a_ps", 6), sig("a_hi", 6), sig("a_lo", 6)
        r_ps, r_t, rh_f, rh_hi, rh_lo = (sig(n, 6) for n in ("r_ps", "r_t", "rh_f", "rh_hi", "rh_lo"))
        z_ps, z_t, c_ps, c_t = (sig(n, 6) for n in ("z_ps", "z_t", "c_ps", "c_t"))
        d_f, u_f, h_new, hN_ps = (sig(n, 6) for n in ("d_f", "u_f", "h_new", "hN_ps"))
        y0 = sig("y0", 2)
        tile_ps, etile_ps = sig("tile_ps", len(ATT_TILES)), sig("etile_ps", len(END_TILES))
        LN_NAMES = (("ln_stats", GB), ("ln_aggr", GB), ("ln_ve", 1), ("ln_rstd", 1), ("ln_out", GB))
        ln_att = {n: sig("att_" + n, 2 * c) for n, c in LN_NAMES}
        ln_end = {n: sig("end_" + n, 3 * c) for n, c in LN_NAMES}

        def ln_sig(name, k):
            s = (ln_att if k < 2 else ln_end)[name]
            return s, (k if k < 2 else k - 2) * s.per_group // (2 if k < 2 else 3)

        x_hi, x_lo = sig("x_hi", 2 * KC), sig("x_lo", 2 * KC)
        x3_hi, x3_lo = sig("x3_hi", KC), sig("x3_lo", KC)
        q1_hi, q1_lo, v1_hi, v1_lo = (sig(n, 2) for n in ("q1_hi", "q1_lo", "v1_hi", "v1_lo"))
        rm_f, rm_hi, rm_lo = (sig(n, 1) for n in ("rm_f", "rm_hi", "rm_lo"))
        u1_f, n2_f, rn_f, y1_f = sig("u1_f", GB), sig("n2_f", GB), sig("rn_f", 1), sig("y1_f", GB)
        q2_hi, q2_lo, k2_hi, k2_lo, v2_hi, v2_lo = (sig(n, 2) for n in
                                                    ("q2_hi", "q2_lo", "k2_hi", "k2_lo", "v2_hi", "v2_lo"))
        stacked = sig("stacked", 6 * HC, 16)
        sm_f, nmax_f, ex_f = sig("sm_f", 8), sig("nmax_f", 8), sig("ex_f", 8)
        pT_hi, pT_lo = sig("pT_hi", 8), sig("pT_lo", 8)
        rinv_f, o_f = sig("rinv_f", GB), sig("o_f", GB)
        oT_hi, oT_lo, proj_f = sig("oT_hi", 2), sig("oT_lo", 2), sig("proj_f", 2)
        base_f, baseo_f, y2_f = sig("base_f", 1), sig("baseo_f", 1), sig("y2_f", 1)
        h3_f, h3_hi, h3_lo, bh_f = sig("h3_f", GB), sig("h3_hi", 1), sig("h3_lo", 1), sig("bh_f", 1)
        presum_f, edge_f, enmax_f, eex_f, erinv_f = (sig("presum_f", 1), sig("edge_f", 2), sig("enmax_f", 1),
                                                    sig("eex_f", 1), sig("erinv_f", 1))
        a3_hi, a3_lo, g3_f, m3_f, e3_f, p3_f, y3_f = (sig("a3_hi", 1), sig("a3_lo", 1), sig("g3_f", GB, base=GB),
                                                      sig("m3_f", 1), sig("e3_f", 1), sig("p3_f", 1), sig("y3_f", 1))
        relu_f, lng_f = sig("relu_f", 1), sig("lng_f", 1)
        stored = sig("stored", 1, 16, base=16)

        TILE = {name: i for tiles in (ATT_TILES, END_TILES) for i, name in enumerate(tiles)}
        FREED = {}
        for c in range(2):
            FREED["x1T", c], FREED["x2T", c], FREED["x3T", c] = (x_lo, c + 1), (x_lo, c + 3), (x3_lo, c + 1)
            FREED["q1T", c], FREED["v1", c] = (q1_lo, c + 1), (v1_lo, c + 1)
            FREED["q2T", c], FREED["k2T", c], FREED["v2", c] = (q2_lo, c + 1), (k2_lo, c + 1), (v2_lo, c + 1)
            FREED["oT", c], FREED["proj", c], FREED["out3", c] = (oT_lo, c + 1), (proj_f, c + 1), (g3_f, 2 * c + 2)
        for b in range(GB):
            FREED["out1", b], FREED["head_out", b], FREED["h3", b] = (n2_f, b + 1), (o_f, b + 1), (h3_f, b + 1)
        for s in range(2 * GB):
            FREED["score", s], FREED["probT", s] = (sm_f, s + 1), (pT_lo, s + 1)
        FREED["rel", 0], FREED["edge", 0], FREED["attT", 0] = (rm_f, 1), (presum_f, 1), (a3_lo, 1)

        def tile(name, k):
            return (ST if (name, k) in ATT_TILES else SE)[TILE[name, k] % 2]

        def tile_full(eng, g, name, k):
            s = tile_ps if (name, k) in ATT_TILES else etile_ps
            eng.wait_ge(s.sem, s.at(g, TILE[name, k] + 1))

        def wait(eng, s, g, k):
            eng.wait_ge(s.sem, s.at(g, k))

        def first(g):
            return isinstance(g, int) and g == 0

        passed = sig("passed", 0)

        def gate(eng, s, g, k):
            wait(eng, s, g, k)
            eng.sem_inc(passed.sem, 1)

        stage = {}

        def staged(name, home, cols):
            stage[name] = home.rearrange("p a b -> p (a b)")[:, 0:KC * cols].rearrange("p (k d) -> p k d", k=KC)
            return stage[name]

        LOADS = [(staged("w3", t_reset, 2 * D), w3_w), (staged("w4", t_update, 2 * D), w4_w),
                 (staged("w5", cand, 2 * D), w5_w), (staged("u3", rh2, D), u3_w), (staged("u5", diff, D), u5_w),
                 (staged("Wq", y_end, D), Wq), (staged("Wk", xs[0], D), Wk), (staged("Wv", xs[1], D), Wv),
                 (staged("wp", h3f, D), w_proj), (staged("wg", y, D), W3l)]
        qkv_home = ex[:, :, :].rearrange("p a b -> p (a b)")[:, 0:KC * 3 * D].rearrange("p (k d) -> p k d", k=KC)
        a_bc = u1[:, 0:2, :]
        bias_in = sb("bias_in", [P, 5, KC])
        wr_f, wzr_f, wh_f = o_n[:, 0:2, :], proj_o[:, 0:2, :], base2[:, 0:2, :]
        wa_f = sb("wa_f", [P, KC, 2])
        wa_t = ln_g[:, :, :]
        N_LOADS = len(LOADS) + 1 + 1 + 5 + 3 + 1 + 2
        PREPARED = {}
        PREP_COUNT = 13
        WT = [(adjT, "adj", ADJ_SCALE, N), (WR, "wr", W_SCALE, D), (WZR, "wzr", W_SCALE, D), (WH, "wh", W_SCALE, D),
              (UG, "u3", W_SCALE, D), (UH, "u5", W_SCALE / 2, D), (WV1, "Wv", W_SCALE, D), (WQK, "qk", W_SCALE, D)]
        WN = [(WQ2, qkv_home[:, :, 0:D], W_SCALE * HD ** -0.5), (WK2, qkv_home[:, :, D:2 * D], W_SCALE),
              (WV2, qkv_home[:, :, 2 * D:3 * D], W_SCALE), (WP2, stage["wp"], W_SCALE),
              ((WG[0][:, :, 0:D], WG[1][:, :, 0:D]), stage["wg"], W_SCALE),
              ((WG[0][:, :, D:D + 2], WG[1][:, :, D:D + 2]), wa_f, W_SCALE)]

        block = ctx.enter_context(nc.Block())

        def x_of(g, src):
            return src[bass.ds(g * GB, GB)].rearrange("b n d -> n b d")

        def run_all(eng, name, gru, tail):
            def body(g, streams, more=True):
                for kind, step, k in body_order(name, streams):
                    if kind == "gru" and (more or step != "next_x"):
                        gru(step, k, g + 2)
                    if kind == "att":
                        tail(step, k, g + 1)
                    if kind == "end":
                        tail(step, k, g)

            gru("next_x", 0, -1)
            body(-2, ("gru",))
            body(-1, ("gru", "att"))
            with eng.Fori(0, NG - 3) as g:
                body(g, ("gru", "att", "end"))
            body(NG - 3, ("gru", "att", "end"), more=False)
            body(NG - 2, ("att", "end"))
            body(NG - 1, ("end",))

        @block.sync
        def _(sp):
            nc_dma = [(adj_n[:, :], adj)]
            nc_dma += [(dst, src.rearrange("(k p) d -> p k d", p=P)) for dst, src in LOADS]
            nc_dma += [(qkv_home, w_qkv.rearrange("(k p) d -> p k d", p=P))]
            nc_dma += [(bproj_b[:, :], b_proj.rearrange("(a d) -> a d", a=1).broadcast_to([P, D])),
                       (gamma_b[:, :], ln_gamma.rearrange("(a d) -> a d", a=1).broadcast_to([P, D])),
                       (lnbeta_b[:, :], ln_beta.rearrange("(a d) -> a d", a=1).broadcast_to([P, D])),
                       (beta_b[:, :], beta3l.rearrange("(a d) -> a d", a=1).broadcast_to([P, 1]))]
            nc_dma += [(a_bc[:, i, :], a3l[i * D:(i + 1) * D, :].rearrange("d a -> a d").broadcast_to([P, D]))
                       for i in range(2)]
            with nc.allow_non_contiguous_dma("biases, one element per partition"):
                nc_dma += [(bias_in[:, i, :], v.rearrange("(k p) -> p k", p=P))
                           for i, v in enumerate((w3_b, u3_b, w4_b, w5_b, u5_b))]
                assert len(nc_dma) == N_LOADS
                for dst, src in nc_dma:
                    sp.dma_start(dst, src).then_inc(w_in.sem, 16)

            def load_x(g, first=False):
                if not first:
                    wait(sp, x_kept, g - 1, 1)
                    wait(sp, xT_ps, g - 1, KC)
                    wait(sp, hN_lo, g - 1, 2)
                sp.dma_start(x_in[:, :, :], x_of(g, x)).then_inc(x_loaded.sem, 16)

            def stack(g):
                for j in range(HC):
                    for dst, src, parts, lo_done in ((qst, q2s, (0, 0, 1), q2_lo), (kst, k2s, (0, 1, 0), k2_lo)):
                        if j == 0:
                            wait(sp, lo_done, g, 2)
                        for r, part in enumerate(parts):
                            d = dst[HD * r:HD * (r + 1), :, :].rearrange("p (c j) t -> p c j t", j=HC)[:, :, j, :]
                            sp.dma_start(d, src[part][HD * j:HD * (j + 1), :, :]).then_inc(stacked.sem, 16)

            def store(g):
                wait(sp, ln_end["ln_out"], g, 3 * GB)
                sp.dma_start(x_of(g, out), xs[3][:, :, :]).then_inc(stored.sem, 16)

            stored.setup(sp)
            load_x(0, first=True)
            load_x(1)
            load_x(2)
            stack(0)
            with sp.Fori(0, NG - 3) as g:
                load_x(g + 3)
                stack(g + 1)
                store(g)
            for g in (NG - 3, NG - 2):
                stack(g + 1)
                store(g)
            store(NG - 1)
            wait(sp, stored, NG - 1, 1)

        @block.gpsimd
        def _(pool):
            pool.memset(ident[:, :], 0.0).then_inc(consts.sem, 1)
            pool.memset(half[:, :], -0.5).then_inc(consts.sem, 1)
            pool.wait_ge(consts.sem, 2)
            pool.affine_select(out=ident[:, :], in_=ident[:, :], compare_op=ALU.not_equal, fill=1.0, base=0,
                               pattern=[[-1, P]], channel_multiplier=1).then_inc(consts.sem, 1)
            pool.wait_ge(consts.sem, 3)

            def gru(step, it, g):
                k0 = KC * it
                h = xT if it == 0 else hT
                if step == "next_x":
                    for p in range(2):
                        ps = slice(2 * p, 2 * p + 2)
                        wait(pool, hN_hi, g + 1, p + 1)
                        pool.tensor_tensor(hNs[1][:, ps, :], x_in[:, ps, :], hNs[0][:, ps, :], ALU.subtract)\
                            .then_inc(hN_lo.sem, 1)
                    for c in range(KC):
                        wait(pool, hT_hi, g + 1, c + 1)
                        wait(pool, hT0, g + 1, c + 1)
                        pool.tensor_tensor(hTs[1][:, c, :], xT[:, c, :], hTs[0][:, c, :], ALU.subtract)\
                            .then_inc(hT_lo.sem, 1)
                if step == "gated":
                    for c in range(KC):
                        wait(pool, rh_hi, g, k0 + c + 1)
                        pool.tensor_tensor(rhs_[1][:, c, :], rh2[:, c, :], rhs_[0][:, c, :], ALU.subtract)\
                            .then_inc(rh_lo.sem, 1)
                if step == "candidate":
                    for c in range(KC):
                        wait(pool, c_t, g, k0 + c + 1)
                        pool.tensor_tensor(diff[:, c, :], cand[:, c, :], h[:, c, :], ALU.subtract)\
                            .then_inc(d_f.sem, 1)
                if step == "state" and it + 1 < ITERS:
                    for c in range(KC):
                        wait(pool, hT_hi, g, k0 + KC + c + 1)
                        pool.tensor_tensor(hTs[1][:, c, :], hT[:, c, :], hTs[0][:, c, :], ALU.subtract)\
                            .then_inc(hT_lo.sem, 1)

            def tail(step, k, g):
                if step == "ln":
                    s, n = ln_sig("ln_ve", k)
                    wait(pool, s, g, n + 1)
                    pool.tensor_tensor(rstd[:, k, :], vareps[:, k, :], half[:, 0:GB], ALU.pow)\
                        .then_inc(ln_sig("ln_rstd", k)[0].sem, 1)
                if step == "ln" and k == 2:
                    lb = lnbeta_b[:, :].rearrange("p (a d) -> p a d", a=1).broadcast_to([P, GB, D])
                    pool.tensor_tensor(base2[:, :, :], xs[1][:, :, :], lb, ALU.add).then_inc(base_f.sem, 1)
                    wait(pool, proj_f, g, 2)
                    wait(pool, base_f, g, 1)
                    pool.tensor_tensor(base2[:, :, :], base2[:, :, :], proj_o[:, :, :], ALU.add).then_inc(baseo_f.sem, 1)
                if step == "rel":
                    wait(pool, rm_hi, g, 1)
                    pool.tensor_tensor(vr[1][:, :, D:D + N], rm[:, :].rearrange("p (b n) -> p b n", b=GB),
                                       vr[0][:, :, D:D + N], ALU.subtract).then_inc(rm_lo.sem, 1)
                if step == "mix1":
                    wait(pool, n2_f, g, GB)
                    pool.tensor_tensor(rstd[:, 5, :], norm2[:, :], half[:, 0:GB], ALU.pow).then_inc(rn_f.sem, 1)
                if step == "ln_out" and k == 2:
                    wait(pool, ln_end["ln_out"], g, GB)
                    gb = gamma_b[:, :].rearrange("p (a d) -> p a d", a=1).broadcast_to([P, GB, D])
                    pool.tensor_tensor(ln_g[:, :, :], ln_o[:, :, :], gb, ALU.mult).then_inc(lng_f.sem, 1)
                if step == "edge":
                    wait(pool, h3_hi, g, 1)
                    pool.tensor_tensor(h3s[1][:, :, :], h3f[:, :, 0:D], h3s[0][:, :, :], ALU.subtract)\
                        .then_inc(h3_lo.sem, 1)
                    pool.tensor_scalar(bh[:, :, :], h3f[:, :, 0:D], beta_b[:, 0:1], 0.0, ALU.mult, ALU.add)\
                        .then_inc(bh_f.sem, 1)
                if step == "elu":
                    wait(pool, relu_f, g, 1)
                    pool.tensor_tensor(bh[:, :, :], bh[:, :, :], xs[2][:, :, :], ALU.add).then_inc(p3_f.sem, 1)

            pool.wait_ge(w_in.sem, 16 * N_LOADS)
            pool.wait_ge(wlo.sem, len(WT) + len(WN))
            run_all(pool, "pool", gru, tail)

        @block.tensor
        def _(pe):
            def mm3(dst, lhsT, rhs, first, last, again=False):
                pe.matmul(dst, lhsT[0], rhs[0], start=first, stop=False, skip_group_check=again)
                pe.matmul(dst, lhsT[0], rhs[1], start=False, stop=False, skip_group_check=again)
                return pe.matmul(dst, lhsT[1], rhs[0], start=False, stop=last, skip_group_check=again)

            def pair(t, *idx):
                return t[0][idx], t[1][idx]

            def project(dst, w, c, act, first, last, again=False):
                for k in range(KC):
                    r = mm3(dst, pair(w, slice(None), k, slice(c * P, (c + 1) * P)), pair(act, slice(None), k),
                            first and k == 0, last and k == KC - 1, again)
                return r

            pe.wait_ge(consts.sem, 3)
            pe.wait_ge(w_in.sem, 16 * N_LOADS)
            pe.wait_ge(prep.sem, PREP_COUNT)
            src = dict(stage, wr=wr_f, wzr=wzr_f, wh=wh_f)
            for i, (dst, name, _, cols) in enumerate(WT):
                if i >= 2:
                    pe.wait_ge(wlo.sem, i - 1)
                t = ST[i % 2]
                if name == "adj":
                    r = pe.transpose(t[:, 0:N], adj_n[:, :], ident[:, :])
                elif name == "qk":
                    for dc in range(KC):
                        for e in range(KC):
                            r = pe.matmul(t[:, dc * D:(dc + 1) * D], stage["Wq"][:, e, dc * P:(dc + 1) * P],
                                          stage["Wk"][:, e, :], start=(e == 0), stop=(e == KC - 1))
                else:
                    for k in range(KC):
                        for o in range(KC):
                            r = pe.transpose(t[:, k * D + o * P:k * D + (o + 1) * P],
                                             src[name][:, o, k * P:(k + 1) * P], ident[:, :])
                r.then_inc(wps.sem, 1)
            pe.wait_ge(wlo.sem, len(WT) + len(WN))

            def nodes_to_features(banks, src_n, done):
                for c in range(KC):
                    for b in range(GB):
                        r = pe.transpose(banks[c][:, b * N:(b + 1) * N], src_n[:, b, c * P:(c + 1) * P], ident[:, :])
                    r.then_inc(done.sem, 1)

            def gru(step, it, g):
                k0 = KC * it
                if step == "next_x":
                    wait(pe, x_loaded, g + 1, 1)
                    if not (isinstance(g, int) and g == -1):
                        wait(pe, c_t, g, KC * ITERS)
                    for c in range(KC):
                        for b in range(GB):
                            r = pe.transpose(SA[c][:, b * N:(b + 1) * N], x_in[:, b, c * P:(c + 1) * P], ident[:, :])
                        r.then_inc(xT_ps.sem, 1)
                if step == "spread":
                    if it == 0 and not (isinstance(g, int) and g == 0):
                        wait(pe, y0, g - 1, 2)
                    wait(pe, hN_lo, g, k0 + 2)
                    if it == 0:
                        wait(pe, hT0, g, KC)
                    for c in range(KC):
                        for b in range(GB):
                            r = mm3(SA[c][:, b * N:(b + 1) * N], pair(hNs, slice(None), b, slice(c * P, (c + 1) * P)),
                                    (adjT[0][:, :], adjT[1][:, :]), True, True)
                        r.then_inc(a_ps.sem, 1)
                if step == "keep":
                    wait(pe, hT_lo, g, k0 + 2)
                    for c in range(KC):
                        project(SG[c][:, :], UG, c, hTs, True, False)
                if step == "reset":
                    wait(pe, a_lo, g, k0 + 2)
                    for c in range(KC):
                        project(SG[c][:, :], WR, c, aTs, False, True).then_inc(r_ps.sem, 1)
                if step == "fresh":
                    for c in range(KC):
                        project(SA[c][:, :], WH, c, aTs, True, False)
                if step == "update":
                    for c in range(KC):
                        wait(pe, r_t, g, k0 + c + 1)
                        project(SG[c][:, :], WZR, c, aTs, False, True, again=True).then_inc(z_ps.sem, 1)
                if step == "candidate":
                    wait(pe, rh_lo, g, k0 + 2)
                    for c in range(KC):
                        project(SA[c][:, :], UH, c, rhs_, False, True).then_inc(c_ps.sem, 1)
                if step == "nodes":
                    if it + 1 == ITERS and not (isinstance(g, int) and g == NG - 1):
                        wait(pe, hT0, g + 1, KC)
                    wait(pe, c_t, g, k0 + KC)
                    for c in range(KC):
                        wait(pe, h_new, g, k0 + c + 1)
                        for b in range(GB):
                            r = pe.transpose(SA[b // 2][:, (b % 2) * D + c * P:(b % 2) * D + (c + 1) * P],
                                             hT[:, c, b * N:(b + 1) * N], ident[:, :])
                            if c == KC - 1 and b % 2:
                                r.then_inc(hN_ps.sem, 1)

            def free_bank(name, k, g):
                tiles, i = ATT_TILES if (name, k) in ATT_TILES else END_TILES, TILE[name, k]
                if i >= 2:
                    s, n = FREED[tiles[i - 2]]
                    wait(pe, s, g, n)
                elif tiles is END_TILES or not first(g):
                    s, n = FREED[tiles[max(j for j in range(len(tiles)) if j % 2 == i)]]
                    wait(pe, s, g - 1, n)

            def tail(step, k, g):
                if (step, k) not in TILE:
                    return
                free_bank(step, k, g)
                t = tile(step, k)
                if step in ("x1T", "x2T", "x3T"):
                    layer = int(step[1]) - 1
                    s, n = ln_sig("ln_out", (0, 1, 3)[layer])
                    wait(pe, s, g, n + GB)
                    for b in range(GB):
                        r = pe.transpose(t[:, b * N:(b + 1) * N], xs[layer][:, b, k * P:(k + 1) * P], ident[:, :])
                elif step in ("q1T", "q2T", "k2T"):
                    wait(pe, x_lo, g, 2 if step == "q1T" else 4)
                    r = project(t[:, :], dict(q1T=WQK, q2T=WQ2, k2T=WK2)[step], k, xTs, True, True)
                elif step in ("v1", "v2"):
                    w = WV1 if step == "v1" else WV2
                    for b in range(2):
                        bb = 2 * k + b
                        for kk in range(KC):
                            r = mm3(t[:, b * D:(b + 1) * D], pair(xTs, slice(None), kk, slice(bb * N, (bb + 1) * N)),
                                    pair(w, slice(None), kk), kk == 0, kk == KC - 1)
                elif step == "rel":
                    wait(pe, q1_lo, g, 2)
                    for b in range(GB):
                        cols = slice(b * N, (b + 1) * N)
                        for kk in range(KC):
                            r = mm3(t[:, cols], pair(xTs, slice(None), kk, cols), pair(q1s, slice(None), kk, cols),
                                    kk == 0, kk == KC - 1)
                elif step == "out1":
                    wait(pe, v1_lo, g, 2)
                    wait(pe, rm_lo, g, 1)
                    r = mm3(t[:, 0:D + N], pair(vr, slice(None), k, slice(D, D + N)), pair(vr, slice(None), k), True, True)
                elif step == "score":
                    b, half_ = k // 2, k % 2
                    wait(pe, stacked, g, 6 * HC)
                    for j in range(HC):
                        hh = half_ * HC + j
                        cols = slice(b * N, (b + 1) * N)
                        r = pe.matmul(t[:, j * N:(j + 1) * N], qst[:, hh, cols], kst[:, hh, cols], start=True, stop=True)
                elif step == "probT":
                    wait(pe, ex_f, g, k + 1)
                    for j in range(HC):
                        r = pe.transpose(t[:, j * N:(j + 1) * N], ex[:, k % 4, j * N:(j + 1) * N], ident[:, :])
                elif step == "head_out":
                    wait(pe, pT_lo, g, 2 * k + 2)
                    wait(pe, v2_lo, g, 2)
                    for hh in range(H):
                        r = mm3(t[:, hh * HD:(hh + 1) * HD], pair(pTs, slice(None), k % 2, hh),
                                pair(v2s, slice(None), k, slice(hh * HD, (hh + 1) * HD)), True, True)
                elif step == "oT":
                    wait(pe, o_f, g, GB)
                    for b in range(GB):
                        r = pe.transpose(t[:, b * N:(b + 1) * N], o_n[:, b, k * P:(k + 1) * P], ident[:, :])
                elif step == "proj":
                    wait(pe, oT_lo, g, 2)
                    for b in range(2):
                        bb = 2 * k + b
                        for kk in range(KC):
                            r = mm3(t[:, b * D:(b + 1) * D], pair(oTs, slice(None), kk, slice(bb * N, (bb + 1) * N)),
                                    pair(WP2, slice(None), kk), kk == 0, kk == KC - 1)
                elif step == "h3":
                    wait(pe, x3_lo, g, 2)
                    for kk in range(KC):
                        r = mm3(t[:, 0:D + 2], pair(x3Ts, slice(None), kk, slice(k * N, (k + 1) * N)),
                                pair(WG, slice(None), kk), kk == 0, kk == KC - 1)
                elif step == "edge":
                    wait(pe, h3_f, g, GB)
                    for b in range(GB):
                        r = pe.transpose(t[:, b * N:(b + 1) * N],
                                         h3f[:, b, D + 1:D + 2].broadcast_to([P, P]), ident[:, :])
                elif step == "attT":
                    wait(pe, eex_f, g, 1)
                    for b in range(GB):
                        r = pe.transpose(t[:, b * N:(b + 1) * N], eex[:, b * N:(b + 1) * N], ident[:, :])
                elif step == "out3":
                    wait(pe, a3_lo, g, 1)
                    wait(pe, h3_lo, g, 1)
                    for b in range(2):
                        bb = 2 * k + b
                        r = mm3(t[:, b * D:(b + 1) * D], pair(aT3, slice(None), bb), pair(h3s, slice(None), bb), True, True)
                r.then_inc((tile_ps if (step, k) in ATT_TILES else etile_ps).sem, 1)

            run_all(pe, "pe", gru, tail)

        @block.scalar
        def _(act):
            def scaled(dst, src_, scale, done):
                act.activation(dst, src_, ACT.Copy, scale=scale).then_inc(done.sem, 1)

            for i, (dst, _, scale, cols) in enumerate(WT):
                act.wait_ge(wps.sem, i + 1)
                if cols == N:
                    scaled(dst[0][:, :], ST[i % 2][:, 0:N], scale, whi)
                else:
                    scaled(dst[0][:, :, :], ST[i % 2][:, :].rearrange("p (k d) -> p k d", k=KC), scale, whi)
            act.wait_ge(w_in.sem, 16 * N_LOADS)
            act.wait_ge(prep.sem, PREP_COUNT)
            for dst, src_, scale in WN:
                scaled(dst[0][:, :, :], src_[:, :, :], scale, whi)
            act.wait_ge(wlo.sem, len(WT) + len(WN))

            def gru(step, it, g):
                k0 = KC * it
                if step == "next_x":
                    if not (isinstance(g, int) and g == -1):
                        wait(act, a_ps, g, KC * ITERS)
                    wait(act, x_loaded, g + 1, 1)
                    for p in range(2):
                        act.activation(hNs[0][:, 2 * p:2 * p + 2, :], x_in[:, 2 * p:2 * p + 2, :], ACT.Copy)\
                            .then_inc(hN_hi.sem, 1)
                    for c in range(KC):
                        wait(act, xT_ps, g + 1, c + 1)
                        act.activation(hTs[0][:, c, :], SA[c][:, :], ACT.Copy).then_inc(hT_hi.sem, 1)
                    for c in range(KC):
                        act.activation(xT[:, c, :], SA[c][:, :], ACT.Copy).then_inc(hT0.sem, 1)
                if step == "x_keep":
                    if not (isinstance(g, int) and g == 0):
                        wait(act, y0, g - 1, 2)
                    act.activation(x_keep[:, :, :], x_in[:, :, :], ACT.Copy).then_inc(x_kept.sem, 1)
                if step == "spread":
                    for c in range(KC):
                        wait(act, a_ps, g, k0 + c + 1)
                        scaled(aTs[0][:, c, :], SA[c][:, :], 1 / ADJ_SCALE, a_hi)
                if step == "reset":
                    for c in range(KC):
                        wait(act, r_ps, g, k0 + c + 1)
                        act.activation(t_reset[:, c, :], SG[c][:, :], ACT.Tanh, bias=gru_bias[:, 0, c:c + 1],
                                       scale=0.5 / W_SCALE).then_inc(r_t.sem, 1)
                if step == "update":
                    for c in range(KC):
                        wait(act, z_ps, g, k0 + c + 1)
                        act.activation(t_update[:, c, :], SG[c][:, :], ACT.Tanh, bias=gru_bias[:, 1, c:c + 1],
                                       scale=0.5 / W_SCALE).then_inc(z_t.sem, 1)
                if step == "candidate":
                    for c in range(KC):
                        wait(act, c_ps, g, k0 + c + 1)
                        act.activation(cand[:, c, :], SA[c][:, :], ACT.Tanh, bias=gru_bias[:, 2, c:c + 1],
                                       scale=1 / W_SCALE).then_inc(c_t.sem, 1)
                if step == "state" and it + 1 < ITERS:
                    for c in range(KC):
                        wait(act, h_new, g, k0 + c + 1)
                        act.activation(hTs[0][:, c, :], hT[:, c, :], ACT.Copy).then_inc(hT_hi.sem, 1)
                if step == "nodes" and it + 1 < ITERS:
                    for p in range(2):
                        wait(act, hN_ps, g, k0 + p + 1)
                        act.activation(hNs[0][:, 2 * p:2 * p + 2, :], SA[p][:, :].rearrange("p (b d) -> p b d", b=2),
                                       ACT.Copy).then_inc(hN_hi.sem, 1)

            def tail(step, k, g):
                if step in ("head_out", "proj", "out3"):
                    return
                if (step, k) in TILE:
                    t = tile(step, k)
                    if step not in ("rel", "score"):
                        tile_full(act, g, step, k)
                pairs = slice(2 * k, 2 * k + 2)
                if step in ("x1T", "x2T"):
                    scaled(xTs[0][:, k, :], t[:, :], 1.0, x_hi)
                elif step == "x3T":
                    scaled(x3Ts[0][:, k, :], t[:, :], 1.0, x3_hi)
                elif step == "q1T":
                    scaled(q1s[0][:, k, :], t[:, :], 1 / W_SCALE, q1_hi)
                elif step == "v1":
                    scaled(vr[0][:, pairs, 0:D], t[:, :].rearrange("p (b d) -> p b d", b=2), 1 / W_SCALE, v1_hi)
                elif step == "rel":
                    wait(act, rm_f, g, 1)
                    scaled(vr[0][:, :, D:D + N], rm[:, :].rearrange("p (b n) -> p b n", b=GB), 1.0, rm_hi)
                elif step == "out1":
                    act.activation(u1[:, k, :], t[:, 0:D], ACT.Copy).then_inc(u1_f.sem, 1)
                elif step == "q2T":
                    scaled(q2s[0][:, k, :], t[:, :], 1 / W_SCALE, q2_hi)
                elif step == "k2T":
                    scaled(k2s[0][:, k, :], t[:, :], 1 / W_SCALE, k2_hi)
                elif step == "v2":
                    scaled(v2s[0][:, pairs, :], t[:, :].rearrange("p (b d) -> p b d", b=2), 1 / W_SCALE, v2_hi)
                elif step == "score":
                    wait(act, nmax_f, g, k + 1)
                    for j in range(HC):
                        r = act.activation(ex[:, k % 4, j * N:(j + 1) * N], sm[:, k % 2, j * N:(j + 1) * N], ACT.Exp,
                                           bias=nmax[:, k, j:j + 1], accum_out=rsum[:, k, j:j + 1])
                    r.then_inc(ex_f.sem, 1)
                elif step == "probT":
                    b, half_ = k // 2, k % 2
                    scaled(pTs[0][:, b % 2, half_ * HC:(half_ + 1) * HC, :],
                           t[:, :].rearrange("p (h n) -> p h n", h=HC), 1.0, pT_hi)
                elif step == "oT":
                    scaled(oTs[0][:, k, :], t[:, :], 1.0, oT_hi)
                elif step == "h3":
                    scaled(h3f[:, k, :], t[:, 0:D + 2], 1 / W_SCALE, h3_f)
                elif step == "edge":
                    wait(act, h3_f, g, GB)
                    for b in range(GB):
                        r = act.activation(presum[:, b * N:(b + 1) * N], t[:, b * N:(b + 1) * N], ACT.Identity,
                                           bias=h3f[:, b, D:D + 1])
                    r.then_inc(presum_f.sem, 1)
                elif step == "edge_soft":
                    wait(act, enmax_f, g, 1)
                    for b in range(GB):
                        r = act.activation(eex[:, b * N:(b + 1) * N], edge[:, b * N:(b + 1) * N], ACT.Exp,
                                           bias=enmax[:, b:b + 1], accum_out=ersum[:, b:b + 1])
                    r.then_inc(eex_f.sem, 1)
                elif step == "attT":
                    scaled(aT3[0][:, :, :], t[:, :].rearrange("p (b n) -> p b n", b=GB), 1.0, a3_hi)
                elif step == "elu":
                    wait(act, g3_f, g, GB)
                    act.activation(bh[:, :, :], g3[:, :, :], ACT.Relu).then_inc(relu_f.sem, 1)
                    wait(act, m3_f, g, 1)
                    act.activation(e3[:, :, :], m3[:, :, :], ACT.Exp).then_inc(e3_f.sem, 1)

            run_all(act, "act", gru, tail)

        @block.vector
        def _(dve):
            def low(dst, src_, scale, hi, done):
                dve.scalar_tensor_tensor(out=dst, in0=src_, scalar=scale, in1=hi, op0=ALU.mult, op1=ALU.subtract)\
                    .then_inc(done.sem, 1)

            g3_f.setup(dve)
            dve.wait_ge(w_in.sem, 16 * N_LOADS)
            count = 0

            def prepared(ins):
                nonlocal count
                count += 1
                ins.then_inc(prep.sem, 1)
                return count

            w3f, w4f, w5f = stage["w3"], stage["w4"], stage["w5"]
            prepared(dve.tensor_tensor(wr_f, w4f[:, :, 0:D], w4f[:, :, D:2 * D], ALU.add))
            n = prepared(dve.tensor_tensor(wzr_f, w3f[:, :, 0:D], w3f[:, :, D:2 * D], ALU.add))
            prepared(dve.tensor_tensor(wh_f, w5f[:, :, 0:D], w5f[:, :, D:2 * D], ALU.add))
            dve.wait_ge(prep.sem, n)
            prepared(dve.tensor_tensor(wzr_f, wzr_f, wr_f, ALU.subtract))
            prepared(dve.tensor_scalar(no_edge[:, :], adj_n[:, :], 0.0, NO_EDGE, ALU.is_equal, ALU.mult))
            prepared(dve.tensor_tensor(gru_bias[:, 0, :], bias_in[:, 2, :], bias_in[:, 1, :], ALU.add))
            prepared(dve.tensor_tensor(gru_bias[:, 1, :], bias_in[:, 0, :], bias_in[:, 1, :], ALU.add))
            prepared(dve.tensor_tensor(gru_bias[:, 2, :], bias_in[:, 3, :], bias_in[:, 4, :], ALU.add))
            dve.wait_ge(prep.sem, count)
            prepared(dve.tensor_scalar(gru_bias[:, 0:2, :], gru_bias[:, 0:2, :], 0.5, None, ALU.mult))
            for i in range(2):
                prepared(dve.tensor_tensor(wa_t[:, 2 * i:2 * i + 2, :], stage["wg"],
                                           a_bc[:, i:i + 1, :].broadcast_to([P, KC, D]), ALU.mult))
                dve.wait_ge(prep.sem, count)
                prepared(dve.tensor_reduce(out=wa_f[:, :, i:i + 1], in_=wa_t[:, 2 * i:2 * i + 2, :], op=ALU.add, axis=AX.X))
            assert count == PREP_COUNT
            dve.wait_ge(prep.sem, count)
            for i, (dst, _, scale, cols) in enumerate(WT):
                dve.wait_ge(whi.sem, i + 1)
                if cols == N:
                    low(dst[1][:, :], ST[i % 2][:, 0:N], scale, dst[0][:, :], wlo)
                else:
                    low(dst[1][:, :, :], ST[i % 2][:, :].rearrange("p (k d) -> p k d", k=KC), scale, dst[0][:, :, :], wlo)
            for i, (dst, src_, scale) in enumerate(WN):
                dve.wait_ge(whi.sem, len(WT) + i + 1)
                low(dst[1][:, :, :], src_[:, :, :], scale, dst[0][:, :, :], wlo)
            dve.wait_ge(wlo.sem, len(WT) + len(WN))

            def gru(step, it, g):
                k0 = KC * it
                h = xT if it == 0 else hT
                if step == "spread":
                    for c in range(KC):
                        wait(dve, a_hi, g, k0 + c + 1)
                        low(aTs[1][:, c, :], SA[c][:, :], 1 / ADJ_SCALE, aTs[0][:, c, :], a_lo)
                if step == "gated":
                    if it == 0 and not first(g):
                        wait(dve, ln_att["ln_out"], g - 1, GB)
                    for c in range(KC):
                        wait(dve, r_t, g, k0 + c + 1)
                        dve.scalar_tensor_tensor(out=rh2[:, c, :], in0=t_reset[:, c, :], scalar=1.0, in1=h[:, c, :],
                                                 op0=ALU.add, op1=ALU.mult).then_inc(rh_f.sem, 1)
                        wait(dve, rh_f, g, k0 + c + 1)
                        dve.tensor_copy(rhs_[0][:, c, :], rh2[:, c, :]).then_inc(rh_hi.sem, 1)
                if step == "blend":
                    for c in range(KC):
                        wait(dve, d_f, g, k0 + c + 1)
                        wait(dve, z_t, g, k0 + c + 1)
                        dve.scalar_tensor_tensor(out=diff[:, c, :], in0=t_update[:, c, :], scalar=1.0,
                                                 in1=diff[:, c, :], op0=ALU.add, op1=ALU.mult).then_inc(u_f.sem, 1)
                        wait(dve, u_f, g, k0 + c + 1)
                        dve.scalar_tensor_tensor(out=hT[:, c, :], in0=diff[:, c, :], scalar=0.5, in1=h[:, c, :],
                                                 op0=ALU.mult, op1=ALU.add).then_inc(h_new.sem, 1)
                if step == "nodes":
                    for p in range(2):
                        ps = slice(2 * p, 2 * p + 2)
                        t = SA[p][:, :].rearrange("p (b d) -> p b d", b=2)
                        if it + 1 < ITERS:
                            wait(dve, hN_hi, g, k0 + 2 + p + 1)
                            dve.tensor_tensor(hNs[1][:, ps, :], t, hNs[0][:, ps, :], ALU.subtract)\
                                .then_inc(hN_lo.sem, 1)
                        else:
                            wait(dve, x_kept, g, 1)
                            wait(dve, hN_ps, g, k0 + p + 1)
                            dve.tensor_tensor(gru_out[:, ps, :], t, x_keep[:, ps, :], ALU.add).then_inc(y0.sem, 1)

            norm_of = ((gru_out, xs[0]), (y, xs[1]), (proj_o, ln_o), (y_end, xs[2]), (y_end, xs[3]))
            norm_in = ((y0, 2), (y1_f, GB), (proj_f, 2), (y2_f, 1), (y3_f, 1))

            def tail(step, k, g):
                t = tile(step, k) if (step, k) in TILE else None
                pairs = slice(2 * k, 2 * k + 2)
                if step == "ln":
                    wait(dve, norm_in[k][0], g, norm_in[k][1])
                    st, n = ln_sig("ln_stats", k)
                    for b in range(GB):
                        dve.bn_stats(out=stats[:, k, b, :], in_=norm_of[k][0][:, b, :]).then_inc(st.sem, 1)
                    gate(dve, st, g, n + GB)
                    ag, n = ln_sig("ln_aggr", k)
                    for b in range(GB):
                        dve.bn_aggr(out=meanvar[:, k, b, :], in_=stats[:, k, b, :]).then_inc(ag.sem, 1)
                    wait(dve, ag, g, n + GB)
                    dve.tensor_scalar(vareps[:, k, :], meanvar[:, k, :, 1], EPS, None, ALU.add)\
                        .then_inc(ln_sig("ln_ve", k)[0].sem, 1)
                elif step == "ln_out":
                    if k == 1 and not first(g):
                        wait(dve, base_f, g - 1, 1)
                    s, n = ln_sig("ln_rstd", k)
                    wait(dve, s, g, n + 1)
                    src_, dst = norm_of[k]
                    for b in range(GB):
                        dve.tensor_scalar(dst[:, b, :], src_[:, b, :], meanvar[:, k, b, 0:1], rstd[:, k, b:b + 1],
                                          ALU.subtract, ALU.mult).then_inc(ln_sig("ln_out", k)[0].sem, 1)
                elif step == "x3T":
                    wait(dve, x3_hi, g, k + 1)
                    low(x3Ts[1][:, k, :], t[:, :], 1.0, x3Ts[0][:, k, :], x3_lo)
                elif step in ("x1T", "x2T"):
                    wait(dve, x_hi, g, 2 * (int(step[1]) - 1) + k + 1)
                    low(xTs[1][:, k, :], t[:, :], 1.0, xTs[0][:, k, :], x_lo)
                elif step == "q1T":
                    wait(dve, q1_hi, g, k + 1)
                    low(q1s[1][:, k, :], t[:, :], 1 / W_SCALE, q1s[0][:, k, :], q1_lo)
                elif step == "v1":
                    wait(dve, v1_hi, g, k + 1)
                    low(vr[1][:, pairs, 0:D], t[:, :].rearrange("p (b d) -> p b d", b=2), 1 / W_SCALE,
                        vr[0][:, pairs, 0:D], v1_lo)
                elif step == "rel":
                    tile_full(dve, g, step, k)
                    rmv = rm[:, :].rearrange("p (b n) -> p b n", b=GB)
                    ab = adj_n[:, :].rearrange("p (a n) -> p a n", a=1).broadcast_to([P, GB, N])
                    dve.tensor_tensor(rmv, t[:, :].rearrange("p (b n) -> p b n", b=GB), ab, ALU.mult)\
                        .then_inc(rm_f.sem, 1)
                elif step == "out1":
                    wait(dve, u1_f, g, k + 1)
                    if k:
                        wait(dve, n2_f, g, k)
                    dve.scalar_tensor_tensor(out=junk[:, :], in0=t[:, D:D + N], scalar=1.0, in1=ident[:, :],
                                             op0=ALU.mult, op1=ALU.mult, accum_out=norm2[:, k:k + 1])\
                        .then_inc(n2_f.sem, 1)
                elif step == "mix1":
                    wait(dve, rn_f, g, 1)
                    for b in range(GB):
                        dve.scalar_tensor_tensor(out=y[:, b, :], in0=u1[:, b, :], scalar=rstd[:, 5, b:b + 1],
                                                 in1=xs[0][:, b, :], op0=ALU.mult, op1=ALU.add).then_inc(y1_f.sem, 1)
                elif step == "q2T":
                    wait(dve, q2_hi, g, k + 1)
                    low(q2s[1][:, k, :], t[:, :], 1 / W_SCALE, q2s[0][:, k, :], q2_lo)
                elif step == "k2T":
                    wait(dve, k2_hi, g, k + 1)
                    low(k2s[1][:, k, :], t[:, :], 1 / W_SCALE, k2s[0][:, k, :], k2_lo)
                elif step == "v2":
                    wait(dve, v2_hi, g, k + 1)
                    low(v2s[1][:, pairs, :], t[:, :].rearrange("p (b d) -> p b d", b=2), 1 / W_SCALE,
                        v2s[0][:, pairs, :], v2_lo)
                elif step == "score":
                    tile_full(dve, g, step, k)
                    if k >= 2:
                        wait(dve, ex_f, g, k - 1)
                    smv = sm[:, k % 2, :].rearrange("p (h m) -> p h m", h=HC)
                    mb = no_edge[:, :].rearrange("p (a m) -> p a m", a=1).broadcast_to([P, HC, N])
                    dve.tensor_tensor(smv, t[:, :].rearrange("p (h m) -> p h m", h=HC), mb, ALU.add)\
                        .then_inc(sm_f.sem, 1)
                    wait(dve, sm_f, g, k + 1)
                    dve.tensor_reduce(out=nmax[:, k, :], in_=smv, op=ALU.max, axis=AX.X, negate=True)\
                        .then_inc(nmax_f.sem, 1)
                elif step == "probT":
                    b, half_ = k // 2, k % 2
                    wait(dve, pT_hi, g, k + 1)
                    hs = slice(half_ * HC, (half_ + 1) * HC)
                    low(pTs[1][:, b % 2, hs, :], t[:, :].rearrange("p (h n) -> p h n", h=HC), 1.0,
                        pTs[0][:, b % 2, hs, :], pT_lo)
                elif step == "head_out":
                    wait(dve, ex_f, g, 2 * k + 2)
                    dve.reciprocal(rinv[:, 2 * k:2 * k + 2, :], rsum[:, 2 * k:2 * k + 2, :]).then_inc(rinv_f.sem, 1)
                    wait(dve, rinv_f, g, k + 1)
                    tile_full(dve, g, step, k)
                    ri = rinv[:, 2 * k:2 * k + 2, :].rearrange("p a (h o) -> p (a h) o", o=1).broadcast_to([P, H, HD])
                    dve.tensor_tensor(o_n[:, k, :].rearrange("p (h d) -> p h d", h=H),
                                      t[:, 0:D].rearrange("p (h d) -> p h d", h=H), ri, ALU.mult).then_inc(o_f.sem, 1)
                elif step == "oT":
                    wait(dve, oT_hi, g, k + 1)
                    low(oTs[1][:, k, :], t[:, :], 1.0, oTs[0][:, k, :], oT_lo)
                elif step == "proj":
                    if not first(g):
                        wait(dve, baseo_f, g - 1, 1)
                        wait(dve, ln_end["ln_out"], g - 1, GB)
                    tile_full(dve, g, step, k)
                    bb = bproj_b[:, :].rearrange("p (a d) -> p a d", a=1).broadcast_to([P, 2, D])
                    dve.scalar_tensor_tensor(out=proj_o[:, pairs, :], in0=t[:, :].rearrange("p (b d) -> p b d", b=2),
                                             scalar=1 / W_SCALE, in1=bb, op0=ALU.mult, op1=ALU.add)\
                        .then_inc(proj_f.sem, 1)
                elif step == "mix2":
                    wait(dve, stored, g - 1, 1)
                    wait(dve, lng_f, g, 1)
                    wait(dve, baseo_f, g, 1)
                    dve.tensor_tensor(y_end[:, :, :], ln_g[:, :, :], base2[:, :, :], ALU.add).then_inc(y2_f.sem, 1)
                elif step == "edge":
                    wait(dve, h3_f, g, GB)
                    dve.tensor_copy(h3s[0][:, :, :], h3f[:, :, 0:D]).then_inc(h3_hi.sem, 1)
                elif step == "edge_soft":
                    wait(dve, presum_f, g, 1)
                    ev = edge[:, :].rearrange("p (b m) -> p b m", b=GB)
                    ab = adj_n[:, :].rearrange("p (a n) -> p a n", a=1).broadcast_to([P, GB, N])
                    dve.scalar_tensor_tensor(out=edge[:, :], in0=presum[:, :], scalar=SLOPE, in1=presum[:, :],
                                             op0=ALU.mult, op1=ALU.max).then_inc(edge_f.sem, 1)
                    wait(dve, edge_f, g, 1)
                    dve.tensor_tensor(ev, ev, ab, ALU.mult).then_inc(edge_f.sem, 1)
                    wait(dve, edge_f, g, 2)
                    dve.tensor_reduce(out=enmax[:, :], in_=ev, op=ALU.max, axis=AX.X, negate=True)\
                        .then_inc(enmax_f.sem, 1)
                elif step == "attT":
                    wait(dve, eex_f, g, 1)
                    dve.reciprocal(erinv[:, :], ersum[:, :]).then_inc(erinv_f.sem, 1)
                    wait(dve, a3_hi, g, 1)
                    low(aT3[1][:, :, :], t[:, :].rearrange("p (b n) -> p b n", b=GB), 1.0, aT3[0][:, :, :], a3_lo)
                elif step == "out3":
                    tile_full(dve, g, step, k)
                    wait(dve, erinv_f, g, 1)
                    wait(dve, bh_f, g, 1)
                    for b in range(2):
                        bb = 2 * k + b
                        dve.scalar_tensor_tensor(out=g3[:, bb, :], in0=t[:, b * D:(b + 1) * D],
                                                 scalar=erinv[:, bb:bb + 1], in1=bh[:, bb, :],
                                                 op0=ALU.mult, op1=ALU.add).then_inc(g3_f.sem, 1)
                elif step == "elu":
                    wait(dve, g3_f, g, GB)
                    dve.tensor_scalar(m3[:, :, :], g3[:, :, :], 0.0, None, ALU.min).then_inc(m3_f.sem, 1)
                    wait(dve, p3_f, g, 1)
                    wait(dve, e3_f, g, 1)
                    dve.scalar_tensor_tensor(out=y_end[:, :, :], in0=e3[:, :, :], scalar=-1.0, in1=bh[:, :, :],
                                             op0=ALU.add, op1=ALU.add).then_inc(y3_f.sem, 1)

            run_all(dve, "dve", gru, tail)


_INS = ['x', 'adj', 'L0_gnn_w3_w', 'L0_gnn_w3_b', 'L0_gnn_u3_w', 'L0_gnn_u3_b', 'L0_gnn_w4_w', 'L0_gnn_w4_b',
        'L0_gnn_w5_w', 'L0_gnn_w5_b', 'L0_gnn_u5_w', 'L0_gnn_u5_b', 'L1_gnn_Wq', 'L1_gnn_Wk', 'L1_gnn_Wv',
        'L2_gnn_w_qkv', 'L2_gnn_w_proj', 'L2_gnn_b_proj', 'L2_gnn_ln_gamma', 'L2_gnn_ln_beta',
        'L3_gnn_W', 'L3_gnn_a', 'L3_gnn_beta']


def kernel(**inputs):
    import numpy as _np
    import concourse.bacc as _bacc
    from concourse import mybir as _mybir
    from concourse.bass_utils import run_bass_kernel_spmd as _run

    nc = _bacc.Bacc("TRN2", target_bir_lowering=False, num_devices=1)
    arrays, args = {}, []
    for name in _INS:
        a = _np.ascontiguousarray(inputs[name])
        arrays[f"in_{name}"] = a
        args.append(nc.dram_tensor(f"in_{name}", a.shape, _mybir.dt.from_np(a.dtype), kind="ExternalInput").ap())
    args.append(nc.dram_tensor("out_x", (B, N, D), F32, kind="ExternalOutput").ap())
    build(nc, *args)
    r = _run(nc, [arrays], core_ids=[0])
    return r.results[0]["out_x"]
```

```python
import concourse.bass as bass
from concourse import mybir
from contextlib import ExitStack

F32 = mybir.dt.float32
F16 = mybir.dt.float16
ALU = mybir.AluOpType
ACT = mybir.ActivationFunctionType
AX = mybir.AxisListType

B, N, D, H = 64, 128, 256, 8
P = 128
GB = 4
NG = B // GB
T = GB * N
KC = D // P
HD = D // H
HC = P // HD
ITERS = 3
EPS = 1e-5
W_SCALE = 16.0
ADJ_SCALE = 64.0
NO_EDGE = -1e30
SLOPE = 0.2

GRU_STEPS = ("spread", "keep", "reset", "gated", "fresh", "update", "candidate", "blend", "state", "nodes")


def gru_steps(more):
    out = []
    for it in range(ITERS):
        for s in GRU_STEPS:
            out.append(("gru", s, it))
            if s == "fresh" and it == 0:
                out.append(("gru", "x_keep", it))
            if s == "candidate" and it == ITERS - 1 and more:
                out.append(("gru", "next_x", it))
    return out


def lin_steps():
    t = [("ln", 0), ("ln_out", 0), ("x1T", 0), ("x1T", 1), ("q1T", 0), ("q1T", 1), ("v1", 0), ("v1", 1), ("rel", 0)]
    t += [("out1", b) for b in range(GB)] + [("mix1", 0), ("ln", 1), ("ln_out", 1)]
    return [("lin",) + s for s in t]


def att_steps():
    t = [("x2T", 0), ("x2T", 1), ("q2T", 0), ("q2T", 1), ("k2T", 0), ("k2T", 1), ("v2", 0), ("v2", 1)]
    t += [("score", 0), ("score", 1), ("score", 2), ("score", 3)]
    for b in range(GB):
        t += [("probT", 2 * b), ("probT", 2 * b + 1), ("head_out", b)]
        if b + 2 < GB:
            t += [("score", 2 * b + 4), ("score", 2 * b + 5)]
    t += [("oT", 0), ("oT", 1), ("proj", 0), ("proj", 1), ("base", 0)]
    return [("att",) + s for s in t]


def end_steps():
    t = [("ln", 2), ("ln_out", 2), ("mix2", 0), ("ln", 3), ("ln_out", 3), ("x3T", 0), ("x3T", 1)]
    t += [("h3", b) for b in range(GB)]
    t += [("edge", 0), ("edge_soft", 0), ("attT", 0), ("out3", 0), ("out3", 1), ("elu", 0), ("ln", 4), ("ln_out", 4)]
    return [("end",) + s for s in t]


NO_TILE = ("ln", "ln_out", "mix1", "mix2", "edge_soft", "elu", "base")
LIN_TILES = [s[1:] for s in lin_steps() if s[1] not in NO_TILE]
ATT_TILES = [s[1:] for s in att_steps() if s[1] not in NO_TILE]
END_TILES = [s[1:] for s in end_steps() if s[1] not in NO_TILE]

MERGE = {
    "pe": "aeeaggallagageaglgglgeggleealeagelaegaeaagaleaggaalaeaegagalagaelg"
          "galeagelaaegalgallgaeaggggagaaggge",
    "dve": "aagelaaelagggaegleglegglegeglagaaalaeageaalgagaageleeaaeglaaaelggg"
           "elgaaglaegaggalaeggaalggelggaaggae",
    "act": "elaeaeggaagegeggaallglglegleaggaeelgagaaeaaaleagaaaaaleggglegeleaa"
           "glaagagllegaaalgelggaaggggggeaagae",
    "pool": "eaggglegglaeegagagealllgagalallagaaaaaaaagggggaeeeleeaeaeagggegaeg"
            "geglaaalaaaaallaeleaagggglgeggggel",
}


def body_order(engine, streams):
    steps = {"g": gru_steps(True), "l": lin_steps(), "a": att_steps(), "e": end_steps()}
    out = [steps[c].pop(0) for c in MERGE[engine]]
    assert not any(steps.values())
    return [s for s in out if s[0] in streams]


class Signal:

    def __init__(self, ctx, nc, name, per_group, step=1, base=0):
        self.sem = ctx.enter_context(nc.semaphore(name))
        self.per_group, self.step = per_group, step
        self.base = base

    def setup(self, eng):
        eng.sem_inc(self.sem, self.base)

    def at(self, g, k):
        return (g * self.per_group + k) * self.step + self.base


def build(nc, x, adj, w3_w, w3_b, u3_w, u3_b, w4_w, w4_b, w5_w, w5_b, u5_w, u5_b, Wq, Wk, Wv,
          w_qkv, w_proj, b_proj, ln_gamma, ln_beta, W3l, a3l, beta3l, out):
    ctx = ExitStack()
    with ctx:
        def sb(name, shape, dt=F32):
            return ctx.enter_context(nc.sbuf_tensor(name, shape, dt))

        def hilo(name, shape):
            return sb(name + "_hi", shape, F16), sb(name + "_lo", shape, F16)

        def sig(name, per_group, step=1, base=0):
            return Signal(ctx, nc, name, per_group, step, base)

        ident = sb("ident", [P, P])
        adj_n = sb("adj_n", [P, N])
        no_edge = sb("no_edge", [P, N])
        half = sb("half", [P, 6 * GB])
        gru_bias = sb("gru_bias", [P, 3, KC])
        bproj_b = sb("bproj_b", [P, D])
        gamma_b = sb("gamma_b", [P, D])
        lnbeta_b = sb("lnbeta_b", [P, D])
        beta_b = sb("beta_b", [P, 1])
        adjT = hilo("adjT", [P, N])
        WR, WZR, WH = hilo("WR", [P, KC, D]), hilo("WZR", [P, KC, D]), hilo("WH", [P, KC, D])
        UG, UH = hilo("UG", [P, KC, D]), hilo("UH", [P, KC, D])
        WQK, WV1 = hilo("WQK", [P, KC, D]), hilo("WV1", [P, KC, D])
        WQ2, WK2, WV2 = hilo("WQ2", [P, KC, D]), hilo("WK2", [P, KC, D]), hilo("WV2", [P, KC, D])
        WP2, WG = hilo("WP2", [P, KC, D]), hilo("WG", [P, KC, D + 2])

        x_in = sb("x_in", [P, GB, D])
        x_keep = sb("x_keep", [P, GB, D])
        hT = sb("hT", [P, KC, T])
        xT = sb("xT", [P, KC, T])
        hTs, hNs = hilo("hTs", [P, KC, T]), hilo("hNs", [P, GB, D])
        aTs, rhs_ = hilo("aTs", [P, KC, T]), hilo("rhTs", [P, KC, T])
        t_reset, t_update = sb("t_reset", [P, KC, T]), sb("t_update", [P, KC, T])
        cand, rh2 = sb("cand", [P, KC, T]), sb("rh2", [P, KC, T])
        diff = cand
        gru_out = rh2[:, :, :].rearrange("p c t -> p (c t)").rearrange("p (b d) -> p b d", b=GB)
        y = sb("y", [P, GB, D])
        y_end = sb("y_end", [P, GB, D])
        xs = [sb("x1", [P, GB, D]), sb("x2", [P, GB, D]), sb("x3", [P, GB, D]), y_end]
        x1Ts, x2Ts, x3Ts = hilo("x1Ts", [P, KC, T]), hilo("x2Ts", [P, KC, T]), hilo("x3Ts", [P, KC, T])
        q1s = hilo("q1s", [P, KC, T])
        vr = hilo("vr", [P, GB, D + N])
        rm = sb("rm", [P, T])
        u1 = sb("u1", [P, GB, D])
        junk = sb("junk", [P, N])
        norm2 = sb("norm2", [P, GB])
        q2s, k2s = hilo("q2s", [P, KC, T]), hilo("k2s", [P, KC, T])
        v2s = hilo("v2s", [P, GB, D])
        qst, kst = sb("qst", [3 * HD, H, T], F16), sb("kst", [3 * HD, H, T], F16)
        sm = sb("sm", [P, 2, HC * N])
        nmax = sb("nmax", [P, 2 * GB, HC])
        rsum = sb("rsum", [P, 2 * GB, HC])
        rinv = sb("rinv", [P, 2 * GB, HC])
        ex = sb("ex", [P, 4, HC * N])
        pTs = hilo("pTs", [P, 2, H, N])
        o_n = sb("o_n", [P, GB, D])
        oTs = x2Ts
        proj_o = sb("proj_o", [P, GB, D])
        base2 = sb("base2", [P, GB, D])
        ln_o = sb("ln_o", [P, GB, D])
        ln_g = sb("ln_g", [P, GB, D])
        h3f = sb("h3f", [P, GB, D + 2])
        h3s = hilo("h3s", [P, GB, D])
        flat_o = ln_o[:, :, :].rearrange("p b d -> p (b d)")
        presum, edge = flat_o[:, 0:T], flat_o[:, T:2 * T]
        enmax, ersum, erinv = sb("enmax", [P, GB]), sb("ersum", [P, GB]), sb("erinv", [P, GB])
        eex = ln_g[:, :, :].rearrange("p b d -> p (b d)")[:, 0:T]
        aT3 = hilo("aT3", [P, GB, N])
        bh = base2
        g3, m3, e3 = y_end, ln_g, ln_o
        stats = sb("stats", [P, 5, GB, 6])
        meanvar = sb("meanvar", [P, 5, GB, 2])
        vareps, rstd = sb("vareps", [P, 6, GB]), sb("rstd", [P, 6, GB])

        def bank(name):
            return ctx.enter_context(nc.psum_tensor(name, [P, 512], F32))
        SA = [bank(f"SA{i}") for i in range(2)]
        SG = [bank(f"SG{i}") for i in range(2)]
        ST = [bank(f"ST{i}") for i in range(2)]
        SL, SE = [bank("SL")], [bank("SE")]

        gnn_in, rest_in, consts = sig("gnn_in", 0, 16), sig("rest_in", 0, 16), sig("consts", 0)
        prep, wps, whi, wlo = sig("prep", 0), sig("wps", 0), sig("whi", 0), sig("wlo", 0)
        x_loaded = sig("x_loaded", 1, 16)
        x_kept = sig("x_kept", 1)
        xT_ps, hT0 = sig("xT_ps", KC), sig("hT0", KC)
        hT_hi, hT_lo = sig("hT_hi", KC * ITERS), sig("hT_lo", KC * ITERS)
        hN_hi, hN_lo = sig("hN_hi", 2 * ITERS), sig("hN_lo", 2 * ITERS)
        a_ps, a_hi, a_lo = sig("a_ps", 6), sig("a_hi", 6), sig("a_lo", 6)
        r_ps, r_t, rh_f, rh_hi, rh_lo = (sig(n, 6) for n in ("r_ps", "r_t", "rh_f", "rh_hi", "rh_lo"))
        z_ps, z_t, c_ps, c_t = (sig(n, 6) for n in ("z_ps", "z_t", "c_ps", "c_t"))
        d_f, u_f, h_new, hN_ps = (sig(n, 6) for n in ("d_f", "u_f", "h_new", "hN_ps"))
        y0 = sig("y0", 2)
        lin_ps, att_ps, end_ps = (sig("lin_ps", len(LIN_TILES)), sig("att_ps", len(ATT_TILES)),
                                  sig("end_ps", len(END_TILES)))
        LN_NAMES = (("ln_stats", GB), ("ln_aggr", GB), ("ln_ve", 1), ("ln_rstd", 1), ("ln_out", GB))
        ln_lin = {n: sig("lin_" + n, 2 * c) for n, c in LN_NAMES}
        ln_end = {n: sig("end_" + n, 3 * c) for n, c in LN_NAMES}

        def ln_sig(name, k):
            s = (ln_lin if k < 2 else ln_end)[name]
            return s, (k if k < 2 else k - 2) * s.per_group // (2 if k < 2 else 3)

        x1_hi, x1_lo = sig("x1_hi", KC), sig("x1_lo", KC)
        x2_hi, x2_lo = sig("x2_hi", KC), sig("x2_lo", KC)
        x3_hi, x3_lo = sig("x3_hi", KC), sig("x3_lo", KC)
        q1_hi, q1_lo, v1_hi, v1_lo = (sig(n, 2) for n in ("q1_hi", "q1_lo", "v1_hi", "v1_lo"))
        rm_f, rm_hi, rm_lo = (sig(n, 1) for n in ("rm_f", "rm_hi", "rm_lo"))
        u1_f, n2_f, rn_f, y1_f = sig("u1_f", GB), sig("n2_f", GB), sig("rn_f", 1), sig("y1_f", GB)
        q2_hi, q2_lo, k2_hi, k2_lo, v2_hi, v2_lo = (sig(n, 2) for n in
                                                    ("q2_hi", "q2_lo", "k2_hi", "k2_lo", "v2_hi", "v2_lo"))
        stacked = sig("stacked", 6 * HC, 16)
        sm_f, nmax_f, ex_f = sig("sm_f", 8), sig("nmax_f", 8), sig("ex_f", 8)
        pT_hi, pT_lo = sig("pT_hi", 8), sig("pT_lo", 8)
        rinv_f, o_f = sig("rinv_f", GB), sig("o_f", GB)
        oT_hi, oT_lo, proj_f = sig("oT_hi", 2), sig("oT_lo", 2), sig("proj_f", 2)
        base_f, baseo_f, y2_f = sig("base_f", 1), sig("baseo_f", 1), sig("y2_f", 1)
        h3_f, h3_hi, h3_lo, bh_f = sig("h3_f", GB), sig("h3_hi", 1), sig("h3_lo", 1), sig("bh_f", 1)
        presum_f, edge_f, enmax_f, eex_f, erinv_f = (sig("presum_f", 1), sig("edge_f", 2), sig("enmax_f", 1),
                                                    sig("eex_f", 1), sig("erinv_f", 1))
        a3_hi, a3_lo, g3_f, m3_f, e3_f, p3_f, y3_f = (sig("a3_hi", 1), sig("a3_lo", 1), sig("g3_f", GB, base=GB),
                                                      sig("m3_f", 1), sig("e3_f", 1), sig("p3_f", 1), sig("y3_f", 1))
        relu_f, lng_f = sig("relu_f", 1), sig("lng_f", 1)
        stored = sig("stored", 1, 16, base=16)

        TILE = {name: (i, tiles, banks, s) for tiles, banks, s in
                ((LIN_TILES, SL, lin_ps), (ATT_TILES, ST, att_ps), (END_TILES, SE, end_ps))
                for i, name in enumerate(tiles)}
        FREED = {}
        for c in range(2):
            FREED["x1T", c], FREED["x2T", c], FREED["x3T", c] = (x1_lo, c + 1), (x2_lo, c + 1), (x3_lo, c + 1)
            FREED["q1T", c], FREED["v1", c] = (q1_lo, c + 1), (v1_lo, c + 1)
            FREED["q2T", c], FREED["k2T", c], FREED["v2", c] = (q2_lo, c + 1), (k2_lo, c + 1), (v2_lo, c + 1)
            FREED["oT", c], FREED["proj", c], FREED["out3", c] = (oT_lo, c + 1), (proj_f, c + 1), (g3_f, 2 * c + 2)
        for b in range(GB):
            FREED["out1", b], FREED["head_out", b], FREED["h3", b] = (n2_f, b + 1), (o_f, b + 1), (h3_f, b + 1)
        for s in range(2 * GB):
            FREED["score", s], FREED["probT", s] = (sm_f, s + 1), (pT_lo, s + 1)
        FREED["rel", 0], FREED["edge", 0], FREED["attT", 0] = (rm_f, 1), (presum_f, 1), (a3_lo, 1)

        def tile(name, k):
            i, _, banks, _ = TILE[name, k]
            return banks[i % len(banks)]

        def tile_full(eng, g, name, k):
            i, _, _, s = TILE[name, k]
            eng.wait_ge(s.sem, s.at(g, i + 1))

        def wait(eng, s, g, k):
            eng.wait_ge(s.sem, s.at(g, k))

        def first(g):
            return isinstance(g, int) and g == 0

        passed = sig("passed", 0)

        def gate(eng, s, g, k):
            wait(eng, s, g, k)
            eng.sem_inc(passed.sem, 1)

        stage = {}

        def staged(name, home, cols):
            stage[name] = home.rearrange("p a b -> p (a b)")[:, 0:KC * cols].rearrange("p (k d) -> p k d", k=KC)
            return stage[name]

        LOADS = [(staged("w3", t_reset, 2 * D), w3_w), (staged("w4", t_update, 2 * D), w4_w),
                 (staged("w5", cand, 2 * D), w5_w), (staged("u3", rh2, D), u3_w), (staged("u5", xs[2], D), u5_w),
                 (staged("Wq", y_end, D), Wq), (staged("Wk", xs[0], D), Wk), (staged("Wv", xs[1], D), Wv),
                 (staged("wp", h3f, D), w_proj), (staged("wg", y, D), W3l)]
        qkv_home = ex[:, :, :].rearrange("p a b -> p (a b)")[:, 0:KC * 3 * D].rearrange("p (k d) -> p k d", k=KC)
        a_bc = u1[:, 0:2, :]
        bias_in = sb("bias_in", [P, 5, KC])
        wr_f, wzr_f, wh_f = o_n[:, 0:2, :], proj_o[:, 0:2, :], base2[:, 0:2, :]
        wa_f = sb("wa_f", [P, KC, 2])
        wa_t = ln_g[:, :, :]
        GNN_LOADS = 1 + 5 + 5
        REST_LOADS = 5 + 1 + 4 + 2
        GNN_PREP, PREP_COUNT = 8, 13
        GNN_WEIGHTS = 6
        WT = [(adjT, "adj", ADJ_SCALE, N), (WR, "wr", W_SCALE, D), (WZR, "wzr", W_SCALE, D), (WH, "wh", W_SCALE, D),
              (UG, "u3", W_SCALE, D), (UH, "u5", W_SCALE / 2, D), (WV1, "Wv", W_SCALE, D), (WQK, "qk", W_SCALE, D)]
        WN = [(WQ2, qkv_home[:, :, 0:D], W_SCALE * HD ** -0.5), (WK2, qkv_home[:, :, D:2 * D], W_SCALE),
              (WV2, qkv_home[:, :, 2 * D:3 * D], W_SCALE), (WP2, stage["wp"], W_SCALE),
              ((WG[0][:, :, 0:D], WG[1][:, :, 0:D]), stage["wg"], W_SCALE),
              ((WG[0][:, :, D:D + 2], WG[1][:, :, D:D + 2]), wa_f, W_SCALE)]

        N_WEIGHTS = len(WT) + len(WN)
        REST = range(GNN_WEIGHTS - 1, N_WEIGHTS)

        block = ctx.enter_context(nc.Block())

        def x_of(g, src):
            return src[bass.ds(g * GB, GB)].rearrange("b n d -> n b d")

        def run_all(eng, name, gru, layers, gnn_weights, rest_weight):
            def body(g, streams, more=True):
                for kind, step, k in body_order(name, streams):
                    if kind == "gru":
                        if more or step != "next_x":
                            gru(step, k, g + 3)
                    else:
                        layers(step, k, g + dict(lin=2, att=1, end=0)[kind])

            gru("next_x", 0, -1)
            gnn_weights()
            rest = list(REST)
            for i, (_, step, k) in enumerate(body_order(name, ("gru",))):
                gru(step, k, 0)
                if i % 3 == 2 and rest:
                    rest_weight(rest.pop(0))
            assert not rest
            eng.wait_ge(wlo.sem, N_WEIGHTS)
            body(-2, ("gru", "lin"))
            body(-1, ("gru", "lin", "att"))
            with eng.Fori(0, NG - 4) as g:
                body(g, ("gru", "lin", "att", "end"))
            body(NG - 4, ("gru", "lin", "att", "end"), more=False)
            body(NG - 3, ("lin", "att", "end"))
            body(NG - 2, ("att", "end"))
            body(NG - 1, ("end",))

        @block.sync
        def _(sp):
            def weights(loads):
                return [(dst, src.rearrange("(k p) d -> p k d", p=P)) for dst, src in loads]

            def load(dmas, count, done):
                assert len(dmas) == count
                for dst, src in dmas:
                    sp.dma_start(dst, src).then_inc(done.sem, 16)

            with nc.allow_non_contiguous_dma("biases, one element per partition"):
                load([(adj_n[:, :], adj)] + weights(LOADS[:5])
                     + [(bias_in[:, i, :], v.rearrange("(k p) -> p k", p=P))
                        for i, v in enumerate((w3_b, u3_b, w4_b, w5_b, u5_b))], GNN_LOADS, gnn_in)
            sp.dma_start(x_in[:, :, :], x_of(0, x)).then_inc(x_loaded.sem, 16)
            rows = [(bproj_b[:, :], b_proj.rearrange("(a d) -> a d", a=1).broadcast_to([P, D])),
                    (gamma_b[:, :], ln_gamma.rearrange("(a d) -> a d", a=1).broadcast_to([P, D])),
                    (lnbeta_b[:, :], ln_beta.rearrange("(a d) -> a d", a=1).broadcast_to([P, D])),
                    (beta_b[:, :], beta3l.rearrange("(a d) -> a d", a=1).broadcast_to([P, 1]))]
            rows += [(a_bc[:, i, :], a3l[i * D:(i + 1) * D, :].rearrange("d a -> a d").broadcast_to([P, D]))
                     for i in range(2)]
            load(weights(LOADS[5:] + [(qkv_home, w_qkv)]) + rows, REST_LOADS, rest_in)

            def load_x(g):
                wait(sp, x_kept, g - 1, 1)
                wait(sp, xT_ps, g - 1, KC)
                wait(sp, hN_lo, g - 1, 2)
                sp.dma_start(x_in[:, :, :], x_of(g, x)).then_inc(x_loaded.sem, 16)

            def stack(g):
                for dst, src, parts, lo_done in ((qst, q2s, (0, 0, 1), q2_lo), (kst, k2s, (0, 1, 0), k2_lo)):
                    wait(sp, lo_done, g, 2)
                    for j in range(HC):
                        for r, part in enumerate(parts):
                            d = dst[HD * r:HD * (r + 1), :, :].rearrange("p (c j) t -> p c j t", j=HC)[:, :, j, :]
                            sp.dma_start(d, src[part][HD * j:HD * (j + 1), :, :]).then_inc(stacked.sem, 16)

            def store(g):
                wait(sp, ln_end["ln_out"], g, 3 * GB)
                sp.dma_start(x_of(g, out), xs[3][:, :, :]).then_inc(stored.sem, 16)

            stored.setup(sp)
            load_x(1)
            load_x(2)
            load_x(3)
            stack(0)
            with sp.Fori(0, NG - 4) as g:
                load_x(g + 4)
                stack(g + 1)
                store(g)
            for g in (NG - 4, NG - 3, NG - 2):
                stack(g + 1)
                store(g)
            store(NG - 1)
            wait(sp, stored, NG - 1, 1)

        @block.gpsimd
        def _(pool):
            pool.memset(ident[:, :], 0.0).then_inc(consts.sem, 1)
            pool.memset(half[:, :], -0.5).then_inc(consts.sem, 1)
            pool.wait_ge(consts.sem, 2)
            pool.affine_select(out=ident[:, :], in_=ident[:, :], compare_op=ALU.not_equal, fill=1.0, base=0,
                               pattern=[[-1, P]], channel_multiplier=1).then_inc(consts.sem, 1)
            pool.wait_ge(consts.sem, 3)

            def gru(step, it, g):
                k0 = KC * it
                h = xT if it == 0 else hT
                if step == "next_x":
                    for p in range(2):
                        ps = slice(2 * p, 2 * p + 2)
                        wait(pool, hN_hi, g + 1, p + 1)
                        pool.tensor_tensor(hNs[1][:, ps, :], x_in[:, ps, :], hNs[0][:, ps, :], ALU.subtract)\
                            .then_inc(hN_lo.sem, 1)
                    for c in range(KC):
                        wait(pool, hT_hi, g + 1, c + 1)
                        wait(pool, hT0, g + 1, c + 1)
                        pool.tensor_tensor(hTs[1][:, c, :], xT[:, c, :], hTs[0][:, c, :], ALU.subtract)\
                            .then_inc(hT_lo.sem, 1)
                if step == "gated":
                    for c in range(KC):
                        wait(pool, rh_hi, g, k0 + c + 1)
                        pool.tensor_tensor(rhs_[1][:, c, :], rh2[:, c, :], rhs_[0][:, c, :], ALU.subtract)\
                            .then_inc(rh_lo.sem, 1)
                if step == "candidate":
                    for c in range(KC):
                        wait(pool, c_t, g, k0 + c + 1)
                        pool.tensor_tensor(diff[:, c, :], cand[:, c, :], h[:, c, :], ALU.subtract)\
                            .then_inc(d_f.sem, 1)
                if step == "state" and it + 1 < ITERS:
                    for c in range(KC):
                        wait(pool, hT_hi, g, k0 + KC + c + 1)
                        pool.tensor_tensor(hTs[1][:, c, :], hT[:, c, :], hTs[0][:, c, :], ALU.subtract)\
                            .then_inc(hT_lo.sem, 1)

            def layers(step, k, g):
                if step == "ln":
                    s, n = ln_sig("ln_ve", k)
                    wait(pool, s, g, n + 1)
                    pool.tensor_tensor(rstd[:, k, :], vareps[:, k, :], half[:, 0:GB], ALU.pow)\
                        .then_inc(ln_sig("ln_rstd", k)[0].sem, 1)
                if step == "base":
                    if not first(g):
                        wait(pool, y3_f, g - 1, 1)
                    wait(pool, ln_lin["ln_out"], g, 2 * GB)
                    lb = lnbeta_b[:, :].rearrange("p (a d) -> p a d", a=1).broadcast_to([P, GB, D])
                    pool.tensor_tensor(base2[:, :, :], xs[1][:, :, :], lb, ALU.add).then_inc(base_f.sem, 1)
                if step == "ln" and k == 2:
                    wait(pool, proj_f, g, 2)
                    wait(pool, base_f, g, 1)
                    pool.tensor_tensor(base2[:, :, :], base2[:, :, :], proj_o[:, :, :], ALU.add).then_inc(baseo_f.sem, 1)
                if step == "rel":
                    wait(pool, rm_hi, g, 1)
                    pool.tensor_tensor(vr[1][:, :, D:D + N], rm[:, :].rearrange("p (b n) -> p b n", b=GB),
                                       vr[0][:, :, D:D + N], ALU.subtract).then_inc(rm_lo.sem, 1)
                if step == "mix1":
                    wait(pool, n2_f, g, GB)
                    pool.tensor_tensor(rstd[:, 5, :], norm2[:, :], half[:, 0:GB], ALU.pow).then_inc(rn_f.sem, 1)
                if step == "ln_out" and k == 2:
                    wait(pool, ln_end["ln_out"], g, GB)
                    gb = gamma_b[:, :].rearrange("p (a d) -> p a d", a=1).broadcast_to([P, GB, D])
                    pool.tensor_tensor(ln_g[:, :, :], ln_o[:, :, :], gb, ALU.mult).then_inc(lng_f.sem, 1)
                if step == "edge":
                    wait(pool, h3_hi, g, 1)
                    pool.tensor_tensor(h3s[1][:, :, :], h3f[:, :, 0:D], h3s[0][:, :, :], ALU.subtract)\
                        .then_inc(h3_lo.sem, 1)
                    pool.tensor_scalar(bh[:, :, :], h3f[:, :, 0:D], beta_b[:, 0:1], 0.0, ALU.mult, ALU.add)\
                        .then_inc(bh_f.sem, 1)
                if step == "elu":
                    wait(pool, relu_f, g, 1)
                    pool.tensor_tensor(bh[:, :, :], bh[:, :, :], xs[2][:, :, :], ALU.add).then_inc(p3_f.sem, 1)

            def gnn_weights():
                pool.wait_ge(wlo.sem, GNN_WEIGHTS)

            run_all(pool, "pool", gru, layers, gnn_weights, lambda i: None)

        @block.tensor
        def _(pe):
            def mm3(dst, lhsT, rhs, first, last, again=False):
                pe.matmul(dst, lhsT[0], rhs[0], start=first, stop=False, skip_group_check=again)
                pe.matmul(dst, lhsT[0], rhs[1], start=False, stop=False, skip_group_check=again)
                return pe.matmul(dst, lhsT[1], rhs[0], start=False, stop=last, skip_group_check=again)

            def pair(t, *idx):
                return t[0][idx], t[1][idx]

            def project(dst, w, c, act, first, last, again=False):
                for k in range(KC):
                    r = mm3(dst, pair(w, slice(None), k, slice(c * P, (c + 1) * P)), pair(act, slice(None), k),
                            first and k == 0, last and k == KC - 1, again)
                return r

            pe.wait_ge(consts.sem, 3)
            src = dict(stage, wr=wr_f, wzr=wzr_f, wh=wh_f)

            def weight(i):
                if i >= len(WT):
                    return
                name, cols = WT[i][1], WT[i][3]
                if i >= 2:
                    pe.wait_ge(wlo.sem, i - 1)
                t = ST[i % 2]
                if name == "adj":
                    r = pe.transpose(t[:, 0:N], adj_n[:, :], ident[:, :])
                elif name == "qk":
                    for dc in range(KC):
                        for e in range(KC):
                            r = pe.matmul(t[:, dc * D:(dc + 1) * D], stage["Wq"][:, e, dc * P:(dc + 1) * P],
                                          stage["Wk"][:, e, :], start=(e == 0), stop=(e == KC - 1))
                else:
                    for k in range(KC):
                        for o in range(KC):
                            r = pe.transpose(t[:, k * D + o * P:k * D + (o + 1) * P],
                                             src[name][:, o, k * P:(k + 1) * P], ident[:, :])
                r.then_inc(wps.sem, 1)

            def gnn_weights():
                pe.wait_ge(gnn_in.sem, 16 * GNN_LOADS)
                pe.wait_ge(prep.sem, GNN_PREP)
                for i in range(GNN_WEIGHTS):
                    weight(i)
                pe.wait_ge(wlo.sem, GNN_WEIGHTS)

            def rest_weight(i):
                if i == REST[0]:
                    pe.wait_ge(rest_in.sem, 16 * REST_LOADS)
                else:
                    weight(i)

            def gru(step, it, g):
                k0 = KC * it
                if step == "next_x":
                    wait(pe, x_loaded, g + 1, 1)
                    if not (isinstance(g, int) and g == -1):
                        wait(pe, c_t, g, KC * ITERS)
                    for c in range(KC):
                        for b in range(GB):
                            r = pe.transpose(SA[c][:, b * N:(b + 1) * N], x_in[:, b, c * P:(c + 1) * P], ident[:, :])
                        r.then_inc(xT_ps.sem, 1)
                if step == "spread":
                    if it == 0 and not (isinstance(g, int) and g == 0):
                        wait(pe, y0, g - 1, 2)
                    wait(pe, hN_lo, g, k0 + 2)
                    if it == 0:
                        wait(pe, hT0, g, KC)
                    for c in range(KC):
                        for b in range(GB):
                            r = mm3(SA[c][:, b * N:(b + 1) * N], pair(hNs, slice(None), b, slice(c * P, (c + 1) * P)),
                                    (adjT[0][:, :], adjT[1][:, :]), True, True)
                        r.then_inc(a_ps.sem, 1)
                if step == "keep":
                    wait(pe, hT_lo, g, k0 + 2)
                    for c in range(KC):
                        project(SG[c][:, :], UG, c, hTs, True, False)
                if step == "reset":
                    wait(pe, a_lo, g, k0 + 2)
                    for c in range(KC):
                        project(SG[c][:, :], WR, c, aTs, False, True).then_inc(r_ps.sem, 1)
                if step == "fresh":
                    for c in range(KC):
                        project(SA[c][:, :], WH, c, aTs, True, False)
                if step == "update":
                    for c in range(KC):
                        wait(pe, r_t, g, k0 + c + 1)
                        project(SG[c][:, :], WZR, c, aTs, False, True, again=True).then_inc(z_ps.sem, 1)
                if step == "candidate":
                    wait(pe, rh_lo, g, k0 + 2)
                    for c in range(KC):
                        project(SA[c][:, :], UH, c, rhs_, False, True).then_inc(c_ps.sem, 1)
                if step == "nodes":
                    if it + 1 == ITERS and not (isinstance(g, int) and g == NG - 1):
                        wait(pe, hT0, g + 1, KC)
                    wait(pe, c_t, g, k0 + KC)
                    for c in range(KC):
                        wait(pe, h_new, g, k0 + c + 1)
                        for b in range(GB):
                            r = pe.transpose(SA[b // 2][:, (b % 2) * D + c * P:(b % 2) * D + (c + 1) * P],
                                             hT[:, c, b * N:(b + 1) * N], ident[:, :])
                            if c == KC - 1 and b % 2:
                                r.then_inc(hN_ps.sem, 1)

            def free_bank(name, k, g):
                i, tiles, banks, _ = TILE[name, k]
                if i >= len(banks):
                    s, n = FREED[tiles[i - len(banks)]]
                    wait(pe, s, g, n)
                elif tiles is END_TILES or not first(g):
                    s, n = FREED[tiles[max(j for j in range(len(tiles)) if j % len(banks) == i)]]
                    wait(pe, s, g - 1, n)

            def layers(step, k, g):
                if (step, k) not in TILE:
                    return
                free_bank(step, k, g)
                t = tile(step, k)
                if step in ("x1T", "x2T", "x3T"):
                    layer = int(step[1]) - 1
                    s, n = ln_sig("ln_out", (0, 1, 3)[layer])
                    wait(pe, s, g, n + GB)
                    for b in range(GB):
                        r = pe.transpose(t[:, b * N:(b + 1) * N], xs[layer][:, b, k * P:(k + 1) * P], ident[:, :])
                elif step in ("q1T", "q2T", "k2T"):
                    wait(pe, x1_lo if step == "q1T" else x2_lo, g, KC)
                    r = project(t[:, :], dict(q1T=WQK, q2T=WQ2, k2T=WK2)[step], k,
                                x1Ts if step == "q1T" else x2Ts, True, True)
                elif step in ("v1", "v2"):
                    w, xt = (WV1, x1Ts) if step == "v1" else (WV2, x2Ts)
                    for b in range(2):
                        bb = 2 * k + b
                        for kk in range(KC):
                            r = mm3(t[:, b * D:(b + 1) * D], pair(xt, slice(None), kk, slice(bb * N, (bb + 1) * N)),
                                    pair(w, slice(None), kk), kk == 0, kk == KC - 1)
                elif step == "rel":
                    wait(pe, q1_lo, g, 2)
                    for b in range(GB):
                        cols = slice(b * N, (b + 1) * N)
                        for kk in range(KC):
                            r = mm3(t[:, cols], pair(x1Ts, slice(None), kk, cols), pair(q1s, slice(None), kk, cols),
                                    kk == 0, kk == KC - 1)
                elif step == "out1":
                    wait(pe, v1_lo, g, 2)
                    wait(pe, rm_lo, g, 1)
                    r = mm3(t[:, 0:D + N], pair(vr, slice(None), k, slice(D, D + N)), pair(vr, slice(None), k), True, True)
                elif step == "score":
                    b, half_ = k // 2, k % 2
                    wait(pe, stacked, g, 6 * HC)
                    for j in range(HC):
                        hh = half_ * HC + j
                        cols = slice(b * N, (b + 1) * N)
                        r = pe.matmul(t[:, j * N:(j + 1) * N], qst[:, hh, cols], kst[:, hh, cols], start=True, stop=True)
                elif step == "probT":
                    wait(pe, ex_f, g, k + 1)
                    for j in range(HC):
                        r = pe.transpose(t[:, j * N:(j + 1) * N], ex[:, k % 4, j * N:(j + 1) * N], ident[:, :])
                elif step == "head_out":
                    wait(pe, pT_lo, g, 2 * k + 2)
                    wait(pe, v2_lo, g, 2)
                    for hh in range(H):
                        r = mm3(t[:, hh * HD:(hh + 1) * HD], pair(pTs, slice(None), k % 2, hh),
                                pair(v2s, slice(None), k, slice(hh * HD, (hh + 1) * HD)), True, True)
                elif step == "oT":
                    wait(pe, o_f, g, GB)
                    for b in range(GB):
                        r = pe.transpose(t[:, b * N:(b + 1) * N], o_n[:, b, k * P:(k + 1) * P], ident[:, :])
                elif step == "proj":
                    wait(pe, oT_lo, g, 2)
                    for b in range(2):
                        bb = 2 * k + b
                        for kk in range(KC):
                            r = mm3(t[:, b * D:(b + 1) * D], pair(oTs, slice(None), kk, slice(bb * N, (bb + 1) * N)),
                                    pair(WP2, slice(None), kk), kk == 0, kk == KC - 1)
                elif step == "h3":
                    wait(pe, x3_lo, g, 2)
                    for kk in range(KC):
                        r = mm3(t[:, 0:D + 2], pair(x3Ts, slice(None), kk, slice(k * N, (k + 1) * N)),
                                pair(WG, slice(None), kk), kk == 0, kk == KC - 1)
                elif step == "edge":
                    wait(pe, h3_f, g, GB)
                    for b in range(GB):
                        r = pe.transpose(t[:, b * N:(b + 1) * N],
                                         h3f[:, b, D + 1:D + 2].broadcast_to([P, P]), ident[:, :])
                elif step == "attT":
                    wait(pe, eex_f, g, 1)
                    for b in range(GB):
                        r = pe.transpose(t[:, b * N:(b + 1) * N], eex[:, b * N:(b + 1) * N], ident[:, :])
                elif step == "out3":
                    wait(pe, a3_lo, g, 1)
                    wait(pe, h3_lo, g, 1)
                    for b in range(2):
                        bb = 2 * k + b
                        r = mm3(t[:, b * D:(b + 1) * D], pair(aT3, slice(None), bb), pair(h3s, slice(None), bb), True, True)
                r.then_inc(TILE[step, k][3].sem, 1)

            run_all(pe, "pe", gru, layers, gnn_weights, rest_weight)

        @block.scalar
        def _(act):
            def scaled(dst, src_, scale, done):
                act.activation(dst, src_, ACT.Copy, scale=scale).then_inc(done.sem, 1)

            def weight(i):
                if i >= len(WT):
                    dst, src_, scale = WN[i - len(WT)]
                    scaled(dst[0][:, :, :], src_[:, :, :], scale, whi)
                    return
                dst, _, scale, cols = WT[i]
                act.wait_ge(wps.sem, i + 1)
                if cols == N:
                    scaled(dst[0][:, :], ST[i % 2][:, 0:N], scale, whi)
                else:
                    scaled(dst[0][:, :, :], ST[i % 2][:, :].rearrange("p (k d) -> p k d", k=KC), scale, whi)

            def gnn_weights():
                for i in range(GNN_WEIGHTS):
                    weight(i)
                act.wait_ge(gnn_in.sem, 16 * GNN_LOADS)
                act.wait_ge(prep.sem, GNN_PREP)
                act.wait_ge(wlo.sem, GNN_WEIGHTS)

            def rest_weight(i):
                if i == REST[0]:
                    act.wait_ge(rest_in.sem, 16 * REST_LOADS)
                    act.wait_ge(prep.sem, PREP_COUNT)
                else:
                    weight(i)

            def gru(step, it, g):
                k0 = KC * it
                if step == "next_x":
                    if not (isinstance(g, int) and g == -1):
                        wait(act, a_ps, g, KC * ITERS)
                    wait(act, x_loaded, g + 1, 1)
                    for p in range(2):
                        act.activation(hNs[0][:, 2 * p:2 * p + 2, :], x_in[:, 2 * p:2 * p + 2, :], ACT.Copy)\
                            .then_inc(hN_hi.sem, 1)
                    for c in range(KC):
                        wait(act, xT_ps, g + 1, c + 1)
                        act.activation(hTs[0][:, c, :], SA[c][:, :], ACT.Copy).then_inc(hT_hi.sem, 1)
                    for c in range(KC):
                        act.activation(xT[:, c, :], SA[c][:, :], ACT.Copy).then_inc(hT0.sem, 1)
                if step == "x_keep":
                    if not (isinstance(g, int) and g == 0):
                        wait(act, y0, g - 1, 2)
                    act.activation(x_keep[:, :, :], x_in[:, :, :], ACT.Copy).then_inc(x_kept.sem, 1)
                if step == "spread":
                    for c in range(KC):
                        wait(act, a_ps, g, k0 + c + 1)
                        scaled(aTs[0][:, c, :], SA[c][:, :], 1 / ADJ_SCALE, a_hi)
                if step == "reset":
                    for c in range(KC):
                        wait(act, r_ps, g, k0 + c + 1)
                        act.activation(t_reset[:, c, :], SG[c][:, :], ACT.Tanh, bias=gru_bias[:, 0, c:c + 1],
                                       scale=0.5 / W_SCALE).then_inc(r_t.sem, 1)
                if step == "update":
                    for c in range(KC):
                        wait(act, z_ps, g, k0 + c + 1)
                        act.activation(t_update[:, c, :], SG[c][:, :], ACT.Tanh, bias=gru_bias[:, 1, c:c + 1],
                                       scale=0.5 / W_SCALE).then_inc(z_t.sem, 1)
                if step == "candidate":
                    for c in range(KC):
                        wait(act, c_ps, g, k0 + c + 1)
                        act.activation(cand[:, c, :], SA[c][:, :], ACT.Tanh, bias=gru_bias[:, 2, c:c + 1],
                                       scale=1 / W_SCALE).then_inc(c_t.sem, 1)
                if step == "state" and it + 1 < ITERS:
                    for c in range(KC):
                        wait(act, h_new, g, k0 + c + 1)
                        act.activation(hTs[0][:, c, :], hT[:, c, :], ACT.Copy).then_inc(hT_hi.sem, 1)
                if step == "nodes" and it + 1 < ITERS:
                    for p in range(2):
                        wait(act, hN_ps, g, k0 + p + 1)
                        act.activation(hNs[0][:, 2 * p:2 * p + 2, :], SA[p][:, :].rearrange("p (b d) -> p b d", b=2),
                                       ACT.Copy).then_inc(hN_hi.sem, 1)

            def layers(step, k, g):
                if step in ("head_out", "proj", "out3"):
                    return
                if (step, k) in TILE:
                    t = tile(step, k)
                    if step not in ("rel", "score"):
                        tile_full(act, g, step, k)
                pairs = slice(2 * k, 2 * k + 2)
                if step == "x1T":
                    scaled(x1Ts[0][:, k, :], t[:, :], 1.0, x1_hi)
                elif step == "x2T":
                    scaled(x2Ts[0][:, k, :], t[:, :], 1.0, x2_hi)
                elif step == "x3T":
                    scaled(x3Ts[0][:, k, :], t[:, :], 1.0, x3_hi)
                elif step == "q1T":
                    scaled(q1s[0][:, k, :], t[:, :], 1 / W_SCALE, q1_hi)
                elif step == "v1":
                    scaled(vr[0][:, pairs, 0:D], t[:, :].rearrange("p (b d) -> p b d", b=2), 1 / W_SCALE, v1_hi)
                elif step == "rel":
                    wait(act, rm_f, g, 1)
                    scaled(vr[0][:, :, D:D + N], rm[:, :].rearrange("p (b n) -> p b n", b=GB), 1.0, rm_hi)
                elif step == "out1":
                    act.activation(u1[:, k, :], t[:, 0:D], ACT.Copy).then_inc(u1_f.sem, 1)
                elif step == "q2T":
                    scaled(q2s[0][:, k, :], t[:, :], 1 / W_SCALE, q2_hi)
                elif step == "k2T":
                    scaled(k2s[0][:, k, :], t[:, :], 1 / W_SCALE, k2_hi)
                elif step == "v2":
                    scaled(v2s[0][:, pairs, :], t[:, :].rearrange("p (b d) -> p b d", b=2), 1 / W_SCALE, v2_hi)
                elif step == "score":
                    wait(act, nmax_f, g, k + 1)
                    for j in range(HC):
                        r = act.activation(ex[:, k % 4, j * N:(j + 1) * N], sm[:, k % 2, j * N:(j + 1) * N], ACT.Exp,
                                           bias=nmax[:, k, j:j + 1], accum_out=rsum[:, k, j:j + 1])
                    r.then_inc(ex_f.sem, 1)
                elif step == "probT":
                    b, half_ = k // 2, k % 2
                    scaled(pTs[0][:, b % 2, half_ * HC:(half_ + 1) * HC, :],
                           t[:, :].rearrange("p (h n) -> p h n", h=HC), 1.0, pT_hi)
                elif step == "oT":
                    scaled(oTs[0][:, k, :], t[:, :], 1.0, oT_hi)
                elif step == "h3":
                    scaled(h3f[:, k, :], t[:, 0:D + 2], 1 / W_SCALE, h3_f)
                elif step == "edge":
                    wait(act, h3_f, g, GB)
                    for b in range(GB):
                        r = act.activation(presum[:, b * N:(b + 1) * N], t[:, b * N:(b + 1) * N], ACT.Identity,
                                           bias=h3f[:, b, D:D + 1])
                    r.then_inc(presum_f.sem, 1)
                elif step == "edge_soft":
                    wait(act, enmax_f, g, 1)
                    for b in range(GB):
                        r = act.activation(eex[:, b * N:(b + 1) * N], edge[:, b * N:(b + 1) * N], ACT.Exp,
                                           bias=enmax[:, b:b + 1], accum_out=ersum[:, b:b + 1])
                    r.then_inc(eex_f.sem, 1)
                elif step == "attT":
                    scaled(aT3[0][:, :, :], t[:, :].rearrange("p (b n) -> p b n", b=GB), 1.0, a3_hi)
                elif step == "elu":
                    wait(act, g3_f, g, GB)
                    act.activation(bh[:, :, :], g3[:, :, :], ACT.Relu).then_inc(relu_f.sem, 1)
                    wait(act, m3_f, g, 1)
                    act.activation(e3[:, :, :], m3[:, :, :], ACT.Exp).then_inc(e3_f.sem, 1)

            run_all(act, "act", gru, layers, gnn_weights, rest_weight)

        @block.vector
        def _(dve):
            def low(dst, src_, scale, hi, done):
                dve.scalar_tensor_tensor(out=dst, in0=src_, scalar=scale, in1=hi, op0=ALU.mult, op1=ALU.subtract)\
                    .then_inc(done.sem, 1)

            g3_f.setup(dve)
            count = 0

            def prepared(ins):
                nonlocal count
                count += 1
                ins.then_inc(prep.sem, 1)
                return count

            def weight(i):
                dve.wait_ge(whi.sem, i + 1)
                if i >= len(WT):
                    dst, src_, scale = WN[i - len(WT)]
                    low(dst[1][:, :, :], src_[:, :, :], scale, dst[0][:, :, :], wlo)
                    return
                dst, _, scale, cols = WT[i]
                if cols == N:
                    low(dst[1][:, :], ST[i % 2][:, 0:N], scale, dst[0][:, :], wlo)
                else:
                    low(dst[1][:, :, :], ST[i % 2][:, :].rearrange("p (k d) -> p k d", k=KC), scale, dst[0][:, :, :], wlo)

            def gnn_weights():
                dve.wait_ge(gnn_in.sem, 16 * GNN_LOADS)
                w3f, w4f, w5f = stage["w3"], stage["w4"], stage["w5"]
                prepared(dve.tensor_tensor(wr_f, w4f[:, :, 0:D], w4f[:, :, D:2 * D], ALU.add))
                n = prepared(dve.tensor_tensor(wzr_f, w3f[:, :, 0:D], w3f[:, :, D:2 * D], ALU.add))
                prepared(dve.tensor_tensor(wh_f, w5f[:, :, 0:D], w5f[:, :, D:2 * D], ALU.add))
                dve.wait_ge(prep.sem, n)
                prepared(dve.tensor_tensor(wzr_f, wzr_f, wr_f, ALU.subtract))
                prepared(dve.tensor_tensor(gru_bias[:, 0, :], bias_in[:, 2, :], bias_in[:, 1, :], ALU.add))
                prepared(dve.tensor_tensor(gru_bias[:, 1, :], bias_in[:, 0, :], bias_in[:, 1, :], ALU.add))
                prepared(dve.tensor_tensor(gru_bias[:, 2, :], bias_in[:, 3, :], bias_in[:, 4, :], ALU.add))
                dve.wait_ge(prep.sem, count)
                prepared(dve.tensor_scalar(gru_bias[:, 0:2, :], gru_bias[:, 0:2, :], 0.5, None, ALU.mult))
                assert count == GNN_PREP
                for i in range(GNN_WEIGHTS):
                    weight(i)
                dve.wait_ge(wlo.sem, GNN_WEIGHTS)

            def rest_weight(i):
                if i != REST[0]:
                    weight(i)
                    return
                dve.wait_ge(rest_in.sem, 16 * REST_LOADS)
                prepared(dve.tensor_scalar(no_edge[:, :], adj_n[:, :], 0.0, NO_EDGE, ALU.is_equal, ALU.mult))
                for i in range(2):
                    prepared(dve.tensor_tensor(wa_t[:, 2 * i:2 * i + 2, :], stage["wg"],
                                               a_bc[:, i:i + 1, :].broadcast_to([P, KC, D]), ALU.mult))
                    dve.wait_ge(prep.sem, count)
                    prepared(dve.tensor_reduce(out=wa_f[:, :, i:i + 1], in_=wa_t[:, 2 * i:2 * i + 2, :], op=ALU.add,
                                               axis=AX.X))
                assert count == PREP_COUNT
                dve.wait_ge(prep.sem, count)

            def gru(step, it, g):
                k0 = KC * it
                h = xT if it == 0 else hT
                if step == "spread":
                    for c in range(KC):
                        wait(dve, a_hi, g, k0 + c + 1)
                        low(aTs[1][:, c, :], SA[c][:, :], 1 / ADJ_SCALE, aTs[0][:, c, :], a_lo)
                if step == "gated":
                    if it == 0 and not first(g):
                        wait(dve, ln_lin["ln_out"], g - 1, GB)
                    for c in range(KC):
                        wait(dve, r_t, g, k0 + c + 1)
                        dve.scalar_tensor_tensor(out=rh2[:, c, :], in0=t_reset[:, c, :], scalar=1.0, in1=h[:, c, :],
                                                 op0=ALU.add, op1=ALU.mult).then_inc(rh_f.sem, 1)
                        wait(dve, rh_f, g, k0 + c + 1)
                        dve.tensor_copy(rhs_[0][:, c, :], rh2[:, c, :]).then_inc(rh_hi.sem, 1)
                if step == "blend":
                    for c in range(KC):
                        wait(dve, d_f, g, k0 + c + 1)
                        wait(dve, z_t, g, k0 + c + 1)
                        dve.scalar_tensor_tensor(out=diff[:, c, :], in0=t_update[:, c, :], scalar=1.0,
                                                 in1=diff[:, c, :], op0=ALU.add, op1=ALU.mult).then_inc(u_f.sem, 1)
                        wait(dve, u_f, g, k0 + c + 1)
                        dve.scalar_tensor_tensor(out=hT[:, c, :], in0=diff[:, c, :], scalar=0.5, in1=h[:, c, :],
                                                 op0=ALU.mult, op1=ALU.add).then_inc(h_new.sem, 1)
                if step == "nodes":
                    for p in range(2):
                        ps = slice(2 * p, 2 * p + 2)
                        t = SA[p][:, :].rearrange("p (b d) -> p b d", b=2)
                        if it + 1 < ITERS:
                            wait(dve, hN_hi, g, k0 + 2 + p + 1)
                            dve.tensor_tensor(hNs[1][:, ps, :], t, hNs[0][:, ps, :], ALU.subtract)\
                                .then_inc(hN_lo.sem, 1)
                        else:
                            wait(dve, x_kept, g, 1)
                            wait(dve, hN_ps, g, k0 + p + 1)
                            dve.tensor_tensor(gru_out[:, ps, :], t, x_keep[:, ps, :], ALU.add).then_inc(y0.sem, 1)

            norm_of = ((gru_out, xs[0]), (y, xs[1]), (proj_o, ln_o), (y_end, xs[2]), (y_end, xs[3]))
            norm_in = ((y0, 2), (y1_f, GB), (proj_f, 2), (y2_f, 1), (y3_f, 1))

            def layers(step, k, g):
                t = tile(step, k) if (step, k) in TILE else None
                pairs = slice(2 * k, 2 * k + 2)
                if step == "ln":
                    wait(dve, norm_in[k][0], g, norm_in[k][1])
                    st, n = ln_sig("ln_stats", k)
                    for b in range(GB):
                        dve.bn_stats(out=stats[:, k, b, :], in_=norm_of[k][0][:, b, :]).then_inc(st.sem, 1)
                    gate(dve, st, g, n + GB)
                    ag, n = ln_sig("ln_aggr", k)
                    for b in range(GB):
                        dve.bn_aggr(out=meanvar[:, k, b, :], in_=stats[:, k, b, :]).then_inc(ag.sem, 1)
                    wait(dve, ag, g, n + GB)
                    dve.tensor_scalar(vareps[:, k, :], meanvar[:, k, :, 1], EPS, None, ALU.add)\
                        .then_inc(ln_sig("ln_ve", k)[0].sem, 1)
                elif step == "ln_out":
                    if k == 1 and not first(g):
                        wait(dve, base_f, g - 1, 1)
                        wait(dve, x2_lo, g - 1, KC)
                    s, n = ln_sig("ln_rstd", k)
                    wait(dve, s, g, n + 1)
                    src_, dst = norm_of[k]
                    for b in range(GB):
                        dve.tensor_scalar(dst[:, b, :], src_[:, b, :], meanvar[:, k, b, 0:1], rstd[:, k, b:b + 1],
                                          ALU.subtract, ALU.mult).then_inc(ln_sig("ln_out", k)[0].sem, 1)
                elif step == "x3T":
                    wait(dve, x3_hi, g, k + 1)
                    low(x3Ts[1][:, k, :], t[:, :], 1.0, x3Ts[0][:, k, :], x3_lo)
                elif step == "x1T":
                    wait(dve, x1_hi, g, k + 1)
                    low(x1Ts[1][:, k, :], t[:, :], 1.0, x1Ts[0][:, k, :], x1_lo)
                elif step == "x2T":
                    wait(dve, x2_hi, g, k + 1)
                    low(x2Ts[1][:, k, :], t[:, :], 1.0, x2Ts[0][:, k, :], x2_lo)
                elif step == "q1T":
                    wait(dve, q1_hi, g, k + 1)
                    low(q1s[1][:, k, :], t[:, :], 1 / W_SCALE, q1s[0][:, k, :], q1_lo)
                elif step == "v1":
                    wait(dve, v1_hi, g, k + 1)
                    low(vr[1][:, pairs, 0:D], t[:, :].rearrange("p (b d) -> p b d", b=2), 1 / W_SCALE,
                        vr[0][:, pairs, 0:D], v1_lo)
                elif step == "rel":
                    tile_full(dve, g, step, k)
                    rmv = rm[:, :].rearrange("p (b n) -> p b n", b=GB)
                    ab = adj_n[:, :].rearrange("p (a n) -> p a n", a=1).broadcast_to([P, GB, N])
                    dve.tensor_tensor(rmv, t[:, :].rearrange("p (b n) -> p b n", b=GB), ab, ALU.mult)\
                        .then_inc(rm_f.sem, 1)
                elif step == "out1":
                    wait(dve, u1_f, g, k + 1)
                    if k:
                        wait(dve, n2_f, g, k)
                    dve.scalar_tensor_tensor(out=junk[:, :], in0=t[:, D:D + N], scalar=1.0, in1=ident[:, :],
                                             op0=ALU.mult, op1=ALU.mult, accum_out=norm2[:, k:k + 1])\
                        .then_inc(n2_f.sem, 1)
                elif step == "mix1":
                    wait(dve, rn_f, g, 1)
                    for b in range(GB):
                        dve.scalar_tensor_tensor(out=y[:, b, :], in0=u1[:, b, :], scalar=rstd[:, 5, b:b + 1],
                                                 in1=xs[0][:, b, :], op0=ALU.mult, op1=ALU.add).then_inc(y1_f.sem, 1)
                elif step == "q2T":
                    wait(dve, q2_hi, g, k + 1)
                    low(q2s[1][:, k, :], t[:, :], 1 / W_SCALE, q2s[0][:, k, :], q2_lo)
                elif step == "k2T":
                    wait(dve, k2_hi, g, k + 1)
                    low(k2s[1][:, k, :], t[:, :], 1 / W_SCALE, k2s[0][:, k, :], k2_lo)
                elif step == "v2":
                    wait(dve, v2_hi, g, k + 1)
                    low(v2s[1][:, pairs, :], t[:, :].rearrange("p (b d) -> p b d", b=2), 1 / W_SCALE,
                        v2s[0][:, pairs, :], v2_lo)
                elif step == "score":
                    tile_full(dve, g, step, k)
                    if k >= 2:
                        wait(dve, ex_f, g, k - 1)
                    smv = sm[:, k % 2, :].rearrange("p (h m) -> p h m", h=HC)
                    mb = no_edge[:, :].rearrange("p (a m) -> p a m", a=1).broadcast_to([P, HC, N])
                    dve.tensor_tensor(smv, t[:, :].rearrange("p (h m) -> p h m", h=HC), mb, ALU.add)\
                        .then_inc(sm_f.sem, 1)
                    wait(dve, sm_f, g, k + 1)
                    dve.tensor_reduce(out=nmax[:, k, :], in_=smv, op=ALU.max, axis=AX.X, negate=True)\
                        .then_inc(nmax_f.sem, 1)
                elif step == "probT":
                    b, half_ = k // 2, k % 2
                    wait(dve, pT_hi, g, k + 1)
                    hs = slice(half_ * HC, (half_ + 1) * HC)
                    low(pTs[1][:, b % 2, hs, :], t[:, :].rearrange("p (h n) -> p h n", h=HC), 1.0,
                        pTs[0][:, b % 2, hs, :], pT_lo)
                elif step == "head_out":
                    wait(dve, ex_f, g, 2 * k + 2)
                    dve.reciprocal(rinv[:, 2 * k:2 * k + 2, :], rsum[:, 2 * k:2 * k + 2, :]).then_inc(rinv_f.sem, 1)
                    wait(dve, rinv_f, g, k + 1)
                    tile_full(dve, g, step, k)
                    ri = rinv[:, 2 * k:2 * k + 2, :].rearrange("p a (h o) -> p (a h) o", o=1).broadcast_to([P, H, HD])
                    dve.tensor_tensor(o_n[:, k, :].rearrange("p (h d) -> p h d", h=H),
                                      t[:, 0:D].rearrange("p (h d) -> p h d", h=H), ri, ALU.mult).then_inc(o_f.sem, 1)
                elif step == "oT":
                    wait(dve, oT_hi, g, k + 1)
                    low(oTs[1][:, k, :], t[:, :], 1.0, oTs[0][:, k, :], oT_lo)
                elif step == "proj":
                    if not first(g):
                        wait(dve, baseo_f, g - 1, 1)
                        wait(dve, ln_end["ln_out"], g - 1, GB)
                    tile_full(dve, g, step, k)
                    bb = bproj_b[:, :].rearrange("p (a d) -> p a d", a=1).broadcast_to([P, 2, D])
                    dve.scalar_tensor_tensor(out=proj_o[:, pairs, :], in0=t[:, :].rearrange("p (b d) -> p b d", b=2),
                                             scalar=1 / W_SCALE, in1=bb, op0=ALU.mult, op1=ALU.add)\
                        .then_inc(proj_f.sem, 1)
                elif step == "mix2":
                    wait(dve, stored, g - 1, 1)
                    wait(dve, lng_f, g, 1)
                    wait(dve, baseo_f, g, 1)
                    dve.tensor_tensor(y_end[:, :, :], ln_g[:, :, :], base2[:, :, :], ALU.add).then_inc(y2_f.sem, 1)
                elif step == "edge":
                    wait(dve, h3_f, g, GB)
                    dve.tensor_copy(h3s[0][:, :, :], h3f[:, :, 0:D]).then_inc(h3_hi.sem, 1)
                elif step == "edge_soft":
                    wait(dve, presum_f, g, 1)
                    ev = edge[:, :].rearrange("p (b m) -> p b m", b=GB)
                    ab = adj_n[:, :].rearrange("p (a n) -> p a n", a=1).broadcast_to([P, GB, N])
                    dve.scalar_tensor_tensor(out=edge[:, :], in0=presum[:, :], scalar=SLOPE, in1=presum[:, :],
                                             op0=ALU.mult, op1=ALU.max).then_inc(edge_f.sem, 1)
                    wait(dve, edge_f, g, 1)
                    dve.tensor_tensor(ev, ev, ab, ALU.mult).then_inc(edge_f.sem, 1)
                    wait(dve, edge_f, g, 2)
                    dve.tensor_reduce(out=enmax[:, :], in_=ev, op=ALU.max, axis=AX.X, negate=True)\
                        .then_inc(enmax_f.sem, 1)
                elif step == "attT":
                    wait(dve, eex_f, g, 1)
                    dve.reciprocal(erinv[:, :], ersum[:, :]).then_inc(erinv_f.sem, 1)
                    wait(dve, a3_hi, g, 1)
                    low(aT3[1][:, :, :], t[:, :].rearrange("p (b n) -> p b n", b=GB), 1.0, aT3[0][:, :, :], a3_lo)
                elif step == "out3":
                    tile_full(dve, g, step, k)
                    wait(dve, erinv_f, g, 1)
                    wait(dve, bh_f, g, 1)
                    for b in range(2):
                        bb = 2 * k + b
                        dve.scalar_tensor_tensor(out=g3[:, bb, :], in0=t[:, b * D:(b + 1) * D],
                                                 scalar=erinv[:, bb:bb + 1], in1=bh[:, bb, :],
                                                 op0=ALU.mult, op1=ALU.add).then_inc(g3_f.sem, 1)
                elif step == "elu":
                    wait(dve, g3_f, g, GB)
                    dve.tensor_scalar(m3[:, :, :], g3[:, :, :], 0.0, None, ALU.min).then_inc(m3_f.sem, 1)
                    wait(dve, p3_f, g, 1)
                    wait(dve, e3_f, g, 1)
                    dve.scalar_tensor_tensor(out=y_end[:, :, :], in0=e3[:, :, :], scalar=-1.0, in1=bh[:, :, :],
                                             op0=ALU.add, op1=ALU.add).then_inc(y3_f.sem, 1)

            run_all(dve, "dve", gru, layers, gnn_weights, rest_weight)


_INS = ['x', 'adj', 'L0_gnn_w3_w', 'L0_gnn_w3_b', 'L0_gnn_u3_w', 'L0_gnn_u3_b', 'L0_gnn_w4_w', 'L0_gnn_w4_b',
        'L0_gnn_w5_w', 'L0_gnn_w5_b', 'L0_gnn_u5_w', 'L0_gnn_u5_b', 'L1_gnn_Wq', 'L1_gnn_Wk', 'L1_gnn_Wv',
        'L2_gnn_w_qkv', 'L2_gnn_w_proj', 'L2_gnn_b_proj', 'L2_gnn_ln_gamma', 'L2_gnn_ln_beta',
        'L3_gnn_W', 'L3_gnn_a', 'L3_gnn_beta']


def kernel(**inputs):
    import numpy as _np
    import concourse.bacc as _bacc
    from concourse import mybir as _mybir
    from concourse.bass_utils import run_bass_kernel_spmd as _run

    nc = _bacc.Bacc("TRN2", target_bir_lowering=False, num_devices=1)
    arrays, args = {}, []
    for name in _INS:
        a = _np.ascontiguousarray(inputs[name])
        arrays[f"in_{name}"] = a
        args.append(nc.dram_tensor(f"in_{name}", a.shape, _mybir.dt.from_np(a.dtype), kind="ExternalInput").ap())
    args.append(nc.dram_tensor("out_x", (B, N, D), F32, kind="ExternalOutput").ap())
    build(nc, *args)
    r = _run(nc, [arrays], core_ids=[0])
    return r.results[0]["out_x"]
```
